# Optimizing a Trainium2 kernel written in Bass

```python
import numpy as np
import jax
import jax.numpy as jnp

def _softmax(x, axis=-1):
    return jax.nn.softmax(x, axis=axis)

def _gelu(x):
    return jax.nn.gelu(x, approximate=True)

def _silu(x):
    return jax.nn.silu(x)

def _sigmoid(x):
    return jax.nn.sigmoid(x)

def _layernorm(x, axis=-1, eps=1e-05):
    m = jnp.mean(x, axis=axis, keepdims=True)
    v = jnp.var(x, axis=axis, keepdims=True)
    return (x - m) / jnp.sqrt(v + eps)

def _scatter_add(tgt, idx, src, axis=0):
    return tgt.at[idx].add(src)

def _segment_sum(src, seg, n):
    return jax.ops.segment_sum(src, seg, n)
kernel_name = 'mk_seq_postln_d1_jaxref_r4_ce2c85'

def setup_inputs(seed: int=0):
    np.random.seed(seed)
    _w = jnp.asarray

    def _L0_attn_setup():
        import jax, jax.numpy as jnp
        import numpy as np
        from jax import lax
        D_MODEL = 256
        D_STATE = 16
        D_CONV = 4
        D_INNER = 2 * D_MODEL

        def _selective_scan(u, dt, A, Bm, Cm):
            dA = jnp.exp(jnp.einsum('bld,dn->bldn', dt, A))
            dB = jnp.einsum('bld,bln->bldn', dt, Bm)
            batch, L, D = u.shape
            N = A.shape[1]
            h0 = jnp.zeros((batch, D, N), dtype=u.dtype)

            def step(h, inp):
                dA_i, dB_i, u_i, C_i = inp
                h = dA_i * h + dB_i * u_i[:, :, None]
                y = jnp.einsum('bdn,bn->bd', h, C_i)
                return (h, y)
            xs = (jnp.moveaxis(dA, 1, 0), jnp.moveaxis(dB, 1, 0), jnp.moveaxis(u, 1, 0), jnp.moveaxis(Cm, 1, 0))
            _, ys = lax.scan(step, h0, xs)
            return jnp.moveaxis(ys, 0, 1)
        key = jax.random.key(seed)
        ks = jax.random.split(key, 8)
        s = 0.02
        x = jax.random.normal(ks[0], (2, 256, D_MODEL), dtype=jnp.float32)
        W_in = jax.random.normal(ks[1], (2 * D_INNER, D_MODEL), dtype=jnp.float32) * s
        W_conv = jax.random.normal(ks[2], (D_INNER, 1, D_CONV), dtype=jnp.float32) * s
        b_conv = jnp.zeros((D_INNER,), dtype=jnp.float32)
        W_dt = jax.random.normal(ks[3], (D_INNER, D_INNER), dtype=jnp.float32) * s
        b_dt = jnp.zeros((D_INNER,), dtype=jnp.float32)
        W_B = jax.random.normal(ks[4], (D_STATE, D_INNER), dtype=jnp.float32) * s
        W_C = jax.random.normal(ks[5], (D_STATE, D_INNER), dtype=jnp.float32) * s
        A_log = jnp.log(jnp.tile(jnp.arange(1, D_STATE + 1, dtype=jnp.float32), (D_INNER, 1)))
        W_out = jax.random.normal(ks[6], (D_MODEL, D_INNER), dtype=jnp.float32) * s
        return {'x': x, 'W_in': W_in, 'W_conv': W_conv, 'b_conv': b_conv, 'W_dt': W_dt, 'b_dt': b_dt, 'W_B': W_B, 'W_C': W_C, 'A_log': A_log, 'W_out': W_out}
    _L0_attn_in = _L0_attn_setup()

    def _L0_ffn_setup():
        import jax, jax.numpy as jnp
        import numpy as np
        H = 256
        E = 32
        I = 128
        TOP_K = 6
        IS = 256
        NORM_MIN = 1e-12
        B, S = (2, 256)
        key = jax.random.key(seed)
        ks = jax.random.split(key, 8)
        sc = 0.02
        return {'hidden_states': jax.random.normal(ks[0], (B, S, H), jnp.float32), 'router_weight': jax.random.normal(ks[1], (E, H), jnp.float32) * sc, 'e_score_bias': jnp.zeros((E,), jnp.float32), 'gate_up_proj': jax.random.normal(ks[2], (E, 2 * I, H), jnp.float32) * sc, 'down_proj': jax.random.normal(ks[3], (E, H, I), jnp.float32) * sc, 'shared_gate_w': jax.random.normal(ks[4], (IS, H), jnp.float32) * sc, 'shared_up_w': jax.random.normal(ks[5], (IS, H), jnp.float32) * sc, 'shared_down_w': jax.random.normal(ks[6], (H, IS), jnp.float32) * sc}
    _L0_ffn_in = _L0_ffn_setup()
    _d = {'L0_attn_x': _L0_attn_in['x'], 'L0_attn_W_in': _L0_attn_in['W_in'], 'L0_attn_W_conv': _L0_attn_in['W_conv'], 'L0_attn_b_conv': _L0_attn_in['b_conv'], 'L0_attn_W_dt': _L0_attn_in['W_dt'], 'L0_attn_b_dt': _L0_attn_in['b_dt'], 'L0_attn_W_B': _L0_attn_in['W_B'], 'L0_attn_W_C': _L0_attn_in['W_C'], 'L0_attn_A_log': _L0_attn_in['A_log'], 'L0_attn_W_out': _L0_attn_in['W_out'], 'L0_ffn_router_weight': _L0_ffn_in['router_weight'], 'L0_ffn_e_score_bias': _L0_ffn_in['e_score_bias'], 'L0_ffn_gate_up_proj': _L0_ffn_in['gate_up_proj'], 'L0_ffn_down_proj': _L0_ffn_in['down_proj'], 'L0_ffn_shared_gate_w': _L0_ffn_in['shared_gate_w'], 'L0_ffn_shared_up_w': _L0_ffn_in['shared_up_w'], 'L0_ffn_shared_down_w': _L0_ffn_in['shared_down_w']}
    _x0 = _d['L0_attn_x']
    _d['L0_attn_x'] = jax.random.normal(jax.random.fold_in(jax.random.key(seed), 1), (1, 4096, 256), dtype=_x0.dtype)
    del _x0
    return _d

def reference(L0_attn_x, L0_attn_W_in, L0_attn_W_conv, L0_attn_b_conv, L0_attn_W_dt, L0_attn_b_dt, L0_attn_W_B, L0_attn_W_C, L0_attn_A_log, L0_attn_W_out, L0_ffn_router_weight, L0_ffn_e_score_bias, L0_ffn_gate_up_proj, L0_ffn_down_proj, L0_ffn_shared_gate_w, L0_ffn_shared_up_w, L0_ffn_shared_down_w):

    def _L0_attn_ref(x, W_in, W_conv, b_conv, W_dt, b_dt, W_B, W_C, A_log, W_out):
        import jax, jax.numpy as jnp
        import numpy as np
        from jax import lax
        D_MODEL = 256
        D_STATE = 16
        D_CONV = 4
        D_INNER = 2 * D_MODEL

        def _selective_scan(u, dt, A, Bm, Cm):
            dA = jnp.exp(jnp.einsum('bld,dn->bldn', dt, A))
            dB = jnp.einsum('bld,bln->bldn', dt, Bm)
            batch, L, D = u.shape
            N = A.shape[1]
            h0 = jnp.zeros((batch, D, N), dtype=u.dtype)

            def step(h, inp):
                dA_i, dB_i, u_i, C_i = inp
                h = dA_i * h + dB_i * u_i[:, :, None]
                y = jnp.einsum('bdn,bn->bd', h, C_i)
                return (h, y)
            xs = (jnp.moveaxis(dA, 1, 0), jnp.moveaxis(dB, 1, 0), jnp.moveaxis(u, 1, 0), jnp.moveaxis(Cm, 1, 0))
            _, ys = lax.scan(step, h0, xs)
            return jnp.moveaxis(ys, 0, 1)
        batch, L, _ = x.shape
        xz = x @ W_in.T
        x_in, z = jnp.split(xz, 2, axis=-1)
        xc = jnp.moveaxis(x_in, 1, 2)
        xc = lax.conv_general_dilated(xc, W_conv, (1,), [(D_CONV - 1, 0)], dimension_numbers=('NCH', 'OIH', 'NCH'), feature_group_count=D_INNER)
        xc = xc + b_conv[None, :, None]
        xc = jax.nn.silu(xc)
        x_conv = jnp.moveaxis(xc, 1, 2)
        dt = jax.nn.softplus(x_conv @ W_dt.T + b_dt)
        Bm = x_conv @ W_B.T
        Cm = x_conv @ W_C.T
        A = -jnp.exp(A_log)
        y = _selective_scan(x_conv, dt, A, Bm, Cm)
        out = y * jax.nn.silu(z)
        return out @ W_out.T

    def _L0_ffn_ref(hidden_states, router_weight, e_score_bias, gate_up_proj, down_proj, shared_gate_w, shared_up_w, shared_down_w):
        import jax, jax.numpy as jnp
        import numpy as np
        H = 256
        E = 32
        I = 128
        TOP_K = 6
        IS = 256
        NORM_MIN = 1e-12
        B, S = (2, 256)
        b, s, h = hidden_states.shape
        x = hidden_states.reshape(-1, h)
        T = x.shape[0]
        shared_out = jax.nn.silu(x @ shared_gate_w.T) * (x @ shared_up_w.T) @ shared_down_w.T
        xf = x.astype(jnp.float32)
        router_logits = xf @ router_weight.T
        routing_weights = jax.nn.softmax(router_logits, axis=-1)
        corrected = routing_weights + e_score_bias
        _, top_idx = jax.lax.top_k(corrected, TOP_K)
        top_w = jnp.take_along_axis(routing_weights, top_idx, axis=-1)
        top_w = top_w / jnp.clip(top_w.sum(axis=-1, keepdims=True), NORM_MIN)
        top_w = top_w.astype(x.dtype)
        combine = jnp.zeros((T, E), x.dtype).at[jnp.arange(T)[:, None], top_idx].add(top_w)
        gu = jnp.einsum('th,eih->tei', x, gate_up_proj)
        gate, up = jnp.split(gu, 2, axis=-1)
        hmid = jax.nn.silu(gate) * up
        y = jnp.einsum('tei,ehi->teh', hmid, down_proj)
        out = jnp.einsum('teh,te->th', y, combine) + shared_out
        return out.reshape(b, s, h)
    x = L0_attn_x
    x = _layernorm(x + _L0_attn_ref(x, L0_attn_W_in, L0_attn_W_conv, L0_attn_b_conv, L0_attn_W_dt, L0_attn_b_dt, L0_attn_W_B, L0_attn_W_C, L0_attn_A_log, L0_attn_W_out), axis=-1)
    x = _layernorm(x + _L0_ffn_ref(x, L0_ffn_router_weight, L0_ffn_e_score_bias, L0_ffn_gate_up_proj, L0_ffn_down_proj, L0_ffn_shared_gate_w, L0_ffn_shared_up_w, L0_ffn_shared_down_w), axis=-1)
    return x

_drawn_inputs = setup_inputs


def setup_inputs(seed=0):
    import zlib

    import numpy as np

    out = dict(_drawn_inputs(seed))
    spreads = {'L0_attn_b_conv': (0.0, 0.8),
     'L0_attn_b_dt': (0.0, 0.8),
     'L0_ffn_e_score_bias': (0.0, 0.8)}
    factors = {'L0_attn_W_in': 8.0,
     'L0_attn_W_conv': 8.0,
     'L0_attn_W_dt': 8.0,
     'L0_attn_W_B': 8.0,
     'L0_attn_W_C': 8.0,
     'L0_attn_A_log': 8.0,
     'L0_attn_W_out': 8.0,
     'L0_ffn_router_weight': 8.0,
     'L0_ffn_gate_up_proj': 8.0,
     'L0_ffn_down_proj': 8.0,
     'L0_ffn_shared_gate_w': 3.378,
     'L0_ffn_shared_up_w': 3.342,
     'L0_ffn_shared_down_w': 3.347}
    for name, (base, spread) in spreads.items():
        noise = np.random.default_rng([zlib.crc32(name.encode()), seed]).standard_normal(out[name].shape)
        drawn = base * np.exp(spread * noise) if base else spread * noise
        out[name] = jnp.asarray(drawn.astype(out[name].dtype))
    for name, factor in factors.items():
        out[name] = (out[name] * factor).astype(out[name].dtype)
    return out
```

```python
from contextlib import ExitStack

import concourse.bass as bass
from concourse import mybir

F32 = mybir.dt.float32
BF16 = mybir.dt.bfloat16
ALU = mybir.AluOpType
ACT = mybir.ActivationFunctionType
AX = mybir.AxisListType

P = 128
D = 256
DI = 512
NST = 16
TAPS = 4
L = 4096
CH = 512
NCH = L // CH
KD = D // P
KI = DI // P
TS = CH // P
NT = L // P
E = 32
EI = 128
TOPK = 6
EX = E + 2
LN_EPS = 1e-5
NORM_MIN = 1e-12
BC = 2 * NST

PROLOGUE = [("IN", m) for m in range(KI)] + [("BC", 0)] + [("DT", m) for m in range(KI)] + [("B", 0), ("B", 1)]
EPILOGUE = [("GT", m) for m in range(KI)] + [("OUT", 0), ("OUT", 1)]
STEP_EXTRAS = {
    0: [("IN", 0), ("IN", 1)],
    1: [("IN", 2), ("IN", 3)],
    2: [("GT", m) for m in range(KI)],
    3: [("Z", 0)],
    4: [("Z", 1)],
    5: [("BC", 0)],
    6: [("DT", 0)],
    7: [("DT", 1)],
    8: [("DT", 2)],
    9: [("DT", 3)],
    10: [("Z", 2)],
    11: [("OUT", 0)],
    12: [("OUT", 1)],
    13: [("Z", 3)],
}
AHEAD = {"IN", "BC", "DT"}
BEHIND = {"GT", "OUT"}


def extras(n, ahead, behind):
    return [u for u in STEP_EXTRAS.get(n, [])
            if (ahead or u[0] not in AHEAD) and (behind or u[0] not in BEHIND)]


def body_uses(ahead, behind):
    uses = []
    for n in range(NST):
        if ahead or n + 2 < NST:
            uses.append(("B", n + 2))
        uses += extras(n, ahead, behind)
    return uses


def px_base(c):
    if isinstance(c, int) and c == 0:
        return len(PROLOGUE)
    return len(PROLOGUE) + len(body_uses(True, False)) + (c - 1) * len(body_uses(True, True))


PX_EPILOGUE = px_base(NCH - 1) + len(body_uses(False, True))


def wait(eng, sem, value):
    if isinstance(value, int) and value <= 0:
        return
    eng.wait_ge(sem, value)


def chunks(eng, body):
    body(0, 0, True, False)
    with eng.Fori(0, (NCH - 2) // 2) as i:
        body(2 * i + 1, 1, True, True)
        body(2 * i + 2, 0, True, True)
    body(NCH - 1, 1, False, True)


def mamba(nc, A, xkeep, ident):
    with ExitStack() as ctx:
        def sb(name, shape, dt=F32):
            return ctx.enter_context(nc.sbuf_tensor(name, shape, dt))

        def sem(name):
            return ctx.enter_context(nc.semaphore(name))

        w_in = sb("w_in", [P, KD, 2 * DI])
        w_dt = sb("w_dt", [P, KI, DI])
        w_bc = sb("w_bc", [P, KI, 3 * BC])
        w_out = sb("w_out", [P, KI, D])
        w_conv = sb("w_conv", [P, KI, TAPS])
        b_conv = sb("b_conv", [P, KI])
        b_dt = sb("b_dt", [P, KI])
        a_neg = sb("a_neg", [P, KI, NST])
        sel_f = sb("sel_f", [3 * BC, BC])
        sel = sb("sel", [3 * BC, BC], BF16)
        xT = sb("xT", [P, 2, KD, CH])
        xr = sb("xr", [P, TS, D])
        xin = sb("xin", [P, KI, TAPS - 1 + CH])
        u = sb("u", [P, KI, CH])
        scr = sb("scr", [P, KI, CH])
        vb = sb("vb", [P, KI, CH])
        g = sb("g", [P, TS, DI])
        gT = sb("gT", [P, KI, CH])
        dt = sb("dt", [P, 2, KI, CH])
        dtu = sb("dtu", [P, KI, CH])
        dbu = sb("dbu", [P, 2, KI, CH])
        h = sb("h", [P, 2, KI, CH])
        hc = sb("hc", [P, 2, KI, CH])
        zg = sb("zg", [P, TS, DI])
        thz = sb("thz", [P, DI])
        bb = sb("bb", [P, 2, CH])
        bc3 = sb("bc3", [3 * BC, 2, CH], BF16)
        bcr = sb("bcr", [3 * BC, CH])
        carry = sb("carry", [P, NST, KI])
        stats = sb("stats", [P, TS, 6])
        mv = sb("mv", [P, TS, 2])
        var = sb("var", [P, TS])
        half = sb("half", [P, TS])
        rstd = sb("rstd", [P, TS])
        y_ps = ctx.enter_context(nc.psum_tensor("y_ps", [P, TS, DI], F32))
        da_ps = ctx.enter_context(nc.psum_tensor("da_ps", [P, 2, CH], F32))
        cb_ps = ctx.enter_context(nc.psum_tensor("cb_ps", [P, CH], F32))
        px = ctx.enter_context(nc.psum_tensor("px", [P, CH], F32))

        s_w = sem("weights_landed")
        s_xT = [sem(f"xT_landed{i}") for i in range(2)]
        s_xr = sem("xr_landed")
        px_full = sem("px_full")
        px_free = sem("px_free")
        prep = sem("prep_act")
        prepv = sem("prep_vector")
        conv_step = sem("conv_step")
        head_done = sem("head_done")
        tanh_u = sem("tanh_u_done")
        u_done = sem("u_done")
        bc_hi = sem("bc_hi_done")
        bc_step = sem("bc_step")
        soft_step = sem("softplus_step")
        dt_done = sem("dt_done")
        dtu_done = sem("dtu_done")
        dbu_done = sem("dbu_done")
        da_full = sem("da_full")
        scan_done = sem("scan_done")
        carry_done = sem("carry_done")
        cb_full = sem("cb_full")
        hc_done = sem("hc_done")
        ytr_done = sem("ytr_done")
        tanh_z = sem("tanh_z_done")
        g_done = sem("g_done")
        ln_step = sem("ln_step")
        stats_seen = sem("stats_seen")
        var_done = sem("var_done")
        rstd_done = sem("rstd_done")
        x1_done = sem("x1_done")

        def use(c, kind, arg, ahead, behind):
            return px_base(c) + body_uses(ahead, behind).index((kind, arg))

        block = ctx.enter_context(nc.Block())
        NW = 10

        @block.sync
        def _(sp):
            for dst, src in (
                (w_in[:], A["W_inT"].rearrange("(k p) n -> p k n", p=P)),
                (w_conv[:], A["W_conv"].rearrange("(m p) t -> p m t", p=P)),
                (b_conv[:], A["b_conv"]),
                (b_dt[:], A["b_dt"]),
                (w_bc[:], A["W_BC3T"].rearrange("(k p) n -> p k n", p=P)),
                (a_neg[:], A["A_log"].rearrange("(m p) s -> p m s", p=P)),
                (w_dt[:], A["W_dtT"].rearrange("(k p) n -> p k n", p=P)),
                (sel_f[:], A["sel3"]),
                (ident[:], A["ident"]),
                (w_out[:], A["W_outT"].rearrange("(k p) n -> p k n", p=P)),
            ):
                sp.dma_start(dst, src).then_inc(s_w, 16)
            xT_d = A["xT"].rearrange("(k p) t -> p k t", p=P)
            x_d = A["x"].rearrange("(j p) d -> p j d", p=P)
            sp.dma_start(xT[:, 0], xT_d[:, :, 0:CH]).then_inc(s_xT[0], 16)

            def load_rows(o):
                wait(sp, x1_done, TS * o)
                sp.dma_start(xr[:], x_d[:, bass.ds(o * TS, TS), :]).then_inc(s_xr, 16)

            def body(c, par, ahead, behind):
                if ahead:
                    if not (isinstance(c, int) and c == 0):
                        sp.wait_ge(tanh_z, TS * c)
                    sp.dma_start(xT[:, 1 - par], xT_d[:, :, bass.ds((c + 1) * CH, CH)]).then_inc(s_xT[1 - par], 16)
                if behind:
                    load_rows(c - 1)

            chunks(sp, body)
            load_rows(NCH - 1)
            sp.wait_ge(x1_done, TS * NCH)

        @block.tensor
        def _(pe):
            def proj_in(q, qpar, m, i):
                if m == 0:
                    pe.wait_ge(s_xT[qpar], (q - qpar) * 8 + 16)
                wait(pe, px_free, i)
                for k in range(KD):
                    mm = pe.matmul(px[:], w_in[:, k, m * P:(m + 1) * P], xT[:, qpar, k, :],
                                   start=(k == 0), stop=(k == KD - 1))
                mm.then_inc(px_full, 1)

            def proj_z(par, ts, i):
                wait(pe, px_free, i)
                for k in range(KD):
                    mm = pe.matmul(px[:], xT[:, par, k, ts * P:(ts + 1) * P], w_in[:, k, DI:2 * DI],
                                   start=(k == 0), stop=(k == KD - 1))
                mm.then_inc(px_full, 1)

            def proj_bc(q, i):
                pe.wait_ge(u_done, q + 1)
                wait(pe, px_free, i)
                for k in range(KI):
                    mm = pe.matmul(px[0:3 * BC, :], w_bc[:, k, :], u[:, k, :], start=(k == 0), stop=(k == KI - 1))
                mm.then_inc(px_full, 1)

            def proj_dt(m, i):
                wait(pe, px_free, i)
                for k in range(KI):
                    mm = pe.matmul(px[:], w_dt[:, k, m * P:(m + 1) * P], u[:, k, :],
                                   start=(k == 0), stop=(k == KI - 1))
                mm.then_inc(px_full, 1)

            def spread(out, row, par):
                return pe.matmul(out, sel[:, row:row + 1].to_broadcast([3 * BC, P]), bc3[:, par, :],
                                 start=True, stop=True)

            def spread_b(c, n, par, i):
                if n == 0:
                    pe.wait_ge(bc_step, 3 * (c + 1))
                wait(pe, px_free, i)
                spread(px[:], n, par).then_inc(px_full, 1)

            def spread_c(c, n, par):
                wait(pe, hc_done, NST * c + n)
                spread(cb_ps[:], NST + n, par).then_inc(cb_full, 1)

            def sum_states(c, n):
                pe.wait_ge(hc_done, NST * c + n + 1)
                if n == 0:
                    wait(pe, g_done, TS * c)
                for t in range(TS):
                    for m in range(KI):
                        mm = pe.matmul(y_ps[:, t, m * P:(m + 1) * P], hc[:, n % 2, m, t * P:(t + 1) * P],
                                       ident[:], is_transpose=True, start=(n == 0 and m == 0),
                                       stop=(n == NST - 1 and m == KI - 1), skip_group_check=True)
                mm.then_inc(ytr_done, 1)

            def gate_T(o, m, i):
                if m == 0:
                    pe.wait_ge(g_done, TS * (o + 1))
                wait(pe, px_free, i)
                for t in range(TS):
                    mm = pe.transpose(px[:, t * P:(t + 1) * P], g[:, t, m * P:(m + 1) * P], ident[:])
                mm.then_inc(px_full, 1)

            def proj_out(j, i):
                wait(pe, px_free, i)
                for t in range(2):
                    ts = 2 * j + t
                    for k in range(KI):
                        mm = pe.matmul(px[:, t * D:(t + 1) * D], gT[:, k, ts * P:(ts + 1) * P], w_out[:, k, :],
                                       start=(k == 0), stop=(k == KI - 1))
                mm.then_inc(px_full, 1)

            pe.wait_ge(s_w, 16 * NW)
            pe.wait_ge(prepv, 3)
            for i, (kind, m) in enumerate(PROLOGUE):
                if kind == "IN":
                    proj_in(0, 0, m, i)
                elif kind == "BC":
                    proj_bc(0, i)
                elif kind == "DT":
                    proj_dt(m, i)
                else:
                    spread_b(0, m, 0, i)

            def body(c, par, ahead, behind):
                for n in range(NST):
                    if n + 2 < NST:
                        spread_b(c, n + 2, par, use(c, "B", n + 2, ahead, behind))
                    elif ahead:
                        spread_b(c + 1, n + 2 - NST, 1 - par, use(c, "B", n + 2, ahead, behind))
                    for kind, m in extras(n, ahead, behind):
                        i = use(c, kind, m, ahead, behind)
                        if kind == "IN":
                            proj_in(c + 1, 1 - par, m, i)
                        elif kind == "Z":
                            proj_z(par, m, i)
                        elif kind == "BC":
                            proj_bc(c + 1, i)
                        elif kind == "DT":
                            proj_dt(m, i)
                        elif kind == "GT":
                            gate_T(c - 1, m, i)
                        else:
                            proj_out(m, i)
                    spread_c(c, n, par)
                    if n > 0:
                        sum_states(c, n - 1)
                    elif behind:
                        sum_states(c - 1, NST - 1)

            chunks(pe, body)
            sum_states(NCH - 1, NST - 1)
            for i, (kind, m) in enumerate(EPILOGUE):
                if kind == "GT":
                    gate_T(NCH - 1, m, PX_EPILOGUE + i)
                else:
                    proj_out(m, PX_EPILOGUE + i)

        @block.scalar
        def _(act):
            def copy_in(q, m, i):
                act.wait_ge(px_full, i + 1)
                if m == 0:
                    act.wait_ge(head_done, q + 1)
                act.activation(xin[:, m, TAPS - 1:], px[:], ACT.Copy).then_inc(px_free, 1)

            def u_tanh(q):
                act.wait_ge(conv_step, KI * TAPS * (q + 1))
                act.activation(scr[:], u[:], ACT.Tanh).then_inc(tanh_u, 1)

            def bc_high(q, par, i):
                act.wait_ge(px_full, i + 1)
                act.activation(bc3[:, par, :], px[0:3 * BC, :], ACT.Copy).then_inc(bc_hi, 1)

            def soft_arg(q, m, i):
                act.wait_ge(px_full, i + 1)
                if m == 0:
                    wait(act, dt_done, q)
                act.activation(vb[:, m, :], px[:], ACT.Identity, bias=b_dt[:, m:m + 1]).then_inc(px_free, 1)

            def soft_abs(q, i):
                act.wait_ge(px_free, i + 1)
                act.activation(scr[:], vb[:], ACT.Abs).then_inc(soft_step, 1)

            def soft_exp(q):
                act.wait_ge(soft_step, 3 * q + 1)
                act.activation(scr[:], scr[:], ACT.Exp, scale=-1.0).then_inc(soft_step, 1)

            def soft_log(q):
                act.wait_ge(soft_step, 3 * q + 2)
                act.activation(scr[:], scr[:], ACT.Ln, bias=1.0).then_inc(soft_step, 1)

            def copy_b(c, n, i):
                act.wait_ge(px_full, i + 1)
                wait(act, dbu_done, NST * c + n - 1)
                act.activation(bb[:, n % 2, :], px[:], ACT.Copy).then_inc(px_free, 1)

            def decay(c, par, n, m):
                if n == 0 and m == 0:
                    act.wait_ge(dt_done, c + 1)
                wait(act, scan_done, (NST * c + n) * KI + m - 1)
                act.activation(da_ps[:, m % 2, :], dt[:, par, m, :], ACT.Exp,
                               scale=a_neg[:, m, n:n + 1]).then_inc(da_full, 1)

            def keep_state(c, n):
                act.wait_ge(scan_done, (NST * c + n + 1) * KI)
                act.activation(carry[:, n, :], h[:, n % 2, :, CH - 1], ACT.Copy).then_inc(carry_done, 1)

            def copy_gT(m, i):
                act.wait_ge(px_full, i + 1)
                act.activation(gT[:, m, :], px[:], ACT.Copy).then_inc(px_free, 1)

            def z_tanh(i):
                act.wait_ge(px_full, i + 1)
                act.activation(thz[:], px[:], ACT.Tanh).then_inc(tanh_z, 1)

            act.wait_ge(s_w, 16 * NW)
            act.activation(a_neg[:], a_neg[:], ACT.Exp).then_inc(prep, 1)
            act.wait_ge(prepv, 4)
            for i, (kind, m) in enumerate(PROLOGUE):
                if kind == "IN":
                    copy_in(0, m, i)
                    if m == KI - 1:
                        u_tanh(0)
                elif kind == "BC":
                    bc_high(0, 0, i)
                elif kind == "DT":
                    soft_arg(0, m, i)
                    if m == KI - 1:
                        soft_abs(0, i)
                        soft_exp(0)
                        soft_log(0)
                else:
                    copy_b(0, m, i)

            def body(c, par, ahead, behind):
                for n in range(NST):
                    decay(c, par, n, 0)
                    decay(c, par, n, 1)
                    if n + 2 < NST:
                        copy_b(c, n + 2, use(c, "B", n + 2, ahead, behind))
                    elif ahead:
                        copy_b(c + 1, n + 2 - NST, use(c, "B", n + 2, ahead, behind))
                    for kind, m in extras(n, ahead, behind):
                        i = use(c, kind, m, ahead, behind)
                        if kind == "IN":
                            copy_in(c + 1, m, i)
                        elif kind == "Z":
                            z_tanh(i)
                        elif kind == "BC":
                            bc_high(c + 1, 1 - par, i)
                        elif kind == "DT":
                            soft_arg(c + 1, m, i)
                        elif kind == "GT":
                            copy_gT(m, i)
                    if ahead and n == 4:
                        u_tanh(c + 1)
                    if ahead and n == 10:
                        soft_abs(c + 1, use(c, "DT", KI - 1, ahead, behind))
                    if ahead and n == 11:
                        soft_exp(c + 1)
                    if ahead and n == 12:
                        soft_log(c + 1)
                    decay(c, par, n, 2)
                    decay(c, par, n, 3)
                    keep_state(c, n)

            chunks(act, body)
            for i, (kind, m) in enumerate(EPILOGUE):
                if kind == "GT":
                    copy_gT(m, PX_EPILOGUE + i)

        @block.gpsimd
        def _(pool):
            def times_u(q, qpar):
                pool.wait_ge(dt_done, q + 1)
                wait(pool, dbu_done, NST * q)
                pool.tensor_tensor(dtu[:], dt[:, qpar], u[:], ALU.mult).then_inc(dtu_done, 1)

            def times_b(c, n, ahead, behind):
                if n == 0:
                    pool.wait_ge(dtu_done, c + 1)
                pool.wait_ge(px_free, (use(c, "B", n, ahead, behind) if n >= 2 else px_base(c) - 2 + n) + 1)
                wait(pool, scan_done, KI * (NST * c + n - 1))
                pool.tensor_tensor(dbu[:, n % 2], dtu[:], bb[:, n % 2, :].unsqueeze(1).to_broadcast([P, KI, CH]),
                                   ALU.mult).then_inc(dbu_done, 1)

            def ln_rstd(o):
                pool.wait_ge(var_done, o + 1)
                pool.tensor_tensor(rstd[:], var[:], half[:], ALU.pow).then_inc(rstd_done, 1)

            times_u(0, 0)

            def body(c, par, ahead, behind):
                for n in range(NST):
                    times_b(c, n, ahead, behind)
                    if behind and n == NST - 1:
                        ln_rstd(c - 1)
                    if ahead and n == NST - 1:
                        times_u(c + 1, 1 - par)

            chunks(pool, body)
            ln_rstd(NCH - 1)

        @block.vector
        def _(ve):
            def conv_taps(q, taps):
                for k in taps:
                    for m in range(KI):
                        first = KI * TAPS * q + KI * k + m
                        src = xin[:, m, k:k + CH]
                        if k == 0:
                            if m == 0:
                                wait(ve, dtu_done, q)
                            ve.tensor_scalar(u[:, m, :], src, w_conv[:, m, 0:1], b_conv[:, m:m + 1],
                                             ALU.mult, ALU.add).then_inc(conv_step, 1)
                        else:
                            ve.wait_ge(conv_step, first - KI + 1)
                            ve.scalar_tensor_tensor(u[:, m, :], src, w_conv[:, m, k:k + 1], u[:, m, :],
                                                    ALU.mult, ALU.add).then_inc(conv_step, 1)

            def conv_head(q):
                ve.wait_ge(conv_step, KI * TAPS * (q + 1))
                ve.tensor_copy(xin[:, :, 0:TAPS - 1], xin[:, :, CH:CH + TAPS - 1]).then_inc(head_done, 1)

            def silu_u(q):
                ve.wait_ge(tanh_u, q + 1)
                ve.scalar_tensor_tensor(u[:], scr[:], 1.0, u[:], ALU.add, ALU.mult).then_inc(u_done, 1)

            def bc_parts(q, par, i):
                lo, lo2 = slice(BC, 3 * BC), slice(2 * BC, 3 * BC)
                ve.wait_ge(bc_hi, q + 1)
                for r in (slice(BC, 2 * BC), lo2):
                    last = ve.tensor_tensor(bcr[r], px[r, :], bc3[r, par, :], ALU.subtract)
                last.then_inc(px_free, 1)
                ve.wait_ge(px_free, i + 1)
                for r in (slice(BC, 2 * BC), lo2):
                    last = ve.tensor_copy(bc3[r, par, :], bcr[r])
                last.then_inc(bc_step, 1)
                ve.wait_ge(bc_step, 3 * q + 1)
                ve.tensor_tensor(bcr[lo2], bcr[lo2], bc3[lo2, par, :], ALU.subtract).then_inc(bc_step, 1)
                ve.wait_ge(bc_step, 3 * q + 2)
                ve.tensor_copy(bc3[lo2, par, :], bcr[lo2]).then_inc(bc_step, 1)

            def softplus(q, qpar):
                ve.wait_ge(soft_step, 3 * (q + 1))
                ve.scalar_tensor_tensor(dt[:, qpar], vb[:], 0.0, scr[:], ALU.max, ALU.add).then_inc(dt_done, 1)

            def scans(c, n):
                ve.wait_ge(dbu_done, NST * c + n + 1)
                wait(ve, hc_done, NST * c + n - 1)
                wait(ve, carry_done, NST * c + n - 1)
                for m in range(KI):
                    ve.wait_ge(da_full, KI * (NST * c + n) + m + 1)
                    ve.tensor_tensor_scan(h[:, n % 2, m, :], da_ps[:, m % 2, :], dbu[:, n % 2, m, :],
                                          carry[:, n, m:m + 1], ALU.mult, ALU.add).then_inc(scan_done, 1)

            def times_c(c, n):
                ve.wait_ge(cb_full, NST * c + n + 1)
                ve.wait_ge(scan_done, KI * (NST * c + n + 1))
                wait(ve, ytr_done, NST * c + n - 1)
                ve.tensor_tensor(hc[:, n % 2], h[:, n % 2], cb_ps[:].unsqueeze(1).to_broadcast([P, KI, CH]),
                                 ALU.mult).then_inc(hc_done, 1)

            def gate(o):
                ve.wait_ge(ytr_done, NST * (o + 1))
                for t in range(TS):
                    ve.tensor_tensor(g[:, t, :], y_ps[:, t, :], zg[:, t, :], ALU.mult).then_inc(g_done, 1)

            def silu_z(c, ts, i):
                ve.wait_ge(tanh_z, TS * c + ts + 1)
                ve.scalar_tensor_tensor(zg[:, ts, :], thz[:], 1.0, px[:], ALU.add, ALU.mult).then_inc(px_free, 1)

            def residual(o, j, i):
                ve.wait_ge(px_full, i + 1)
                ve.wait_ge(s_xr, 16 * (o + 1))
                ve.tensor_tensor(xr[:, 2 * j:2 * j + 2, :], px[:].rearrange("p (t d) -> p t d", t=2),
                                 xr[:, 2 * j:2 * j + 2, :], ALU.add).then_inc(px_free, 1)

            def ln_stats(o, i):
                ve.wait_ge(px_free, i + 1)
                for t in range(TS):
                    ve.bn_stats(stats[:, t, :], xr[:, t, :]).then_inc(ln_step, 1)
                ve.wait_ge(ln_step, 2 * TS * o + TS)
                ve.sem_inc(stats_seen, 1)
                for t in range(TS):
                    ve.bn_aggr(mv[:, t, :], stats[:, t, :]).then_inc(ln_step, 1)
                ve.wait_ge(ln_step, 2 * TS * (o + 1))
                ve.tensor_scalar(var[:], mv[:, :, 1], LN_EPS, None, ALU.add).then_inc(var_done, 1)

            def ln_apply(o):
                ve.wait_ge(rstd_done, o + 1)
                for t in range(TS):
                    ve.tensor_scalar(xkeep[:, bass.ds(o * TS + t, 1), :], xr[:, t:t + 1, :], mv[:, t, 0:1], rstd[:, t:t + 1],
                                     ALU.subtract, ALU.mult).then_inc(x1_done, 1)

            ve.memset(xin[:, :, 0:TAPS - 1], 0.0).then_inc(head_done, 1)
            ve.memset(carry[:], 0.0)
            ve.memset(half[:], -0.5)
            ve.wait_ge(s_w, 16 * NW)
            ve.tensor_copy(sel[:], sel_f[:]).then_inc(prepv, 1)
            ve.tensor_scalar(w_in[:, :, DI:], w_in[:, :, DI:], 0.5, None, ALU.mult).then_inc(prepv, 1)
            ve.tensor_scalar(w_conv[:], w_conv[:], 0.5, None, ALU.mult).then_inc(prepv, 1)
            ve.tensor_scalar(b_conv[:], b_conv[:], 0.5, None, ALU.mult)
            ve.wait_ge(prep, 1)
            ve.tensor_scalar(a_neg[:], a_neg[:], -1.0, None, ALU.mult).then_inc(prepv, 1)
            ve.wait_ge(prepv, 4)

            ve.wait_ge(px_free, KI)
            conv_taps(0, range(TAPS))
            conv_head(0)
            silu_u(0)
            bc_parts(0, 0, KI)
            softplus(0, 0)

            def body(c, par, ahead, behind):
                for n in range(NST):
                    scans(c, n)
                    if n == 1 and behind:
                        gate(c - 1)
                    if ahead and n == 2:
                        ve.wait_ge(px_free, use(c, "IN", KI - 1, ahead, behind) + 1)
                        conv_taps(c + 1, (0, 1))
                    if ahead and n == 3:
                        conv_taps(c + 1, (2, 3))
                        conv_head(c + 1)
                    if ahead and n == 4:
                        silu_u(c + 1)
                    for kind, m in extras(n, ahead, behind):
                        i = use(c, kind, m, ahead, behind)
                        if kind == "Z":
                            silu_z(c, m, i)
                        elif kind == "BC":
                            bc_parts(c + 1, 1 - par, i)
                        elif kind == "OUT":
                            residual(c - 1, m, i)
                    if ahead and n == 13:
                        softplus(c + 1, 1 - par)
                    if behind and n == 13:
                        ln_stats(c - 1, use(c, "OUT", 1, ahead, behind))
                    if behind and n == 15:
                        ln_apply(c - 1)
                    if n > 0:
                        times_c(c, n - 1)
                    elif behind:
                        times_c(c - 1, NST - 1)

            chunks(ve, body)
            times_c(NCH - 1, NST - 1)
            gate(NCH - 1)
            for j in range(2):
                residual(NCH - 1, j, PX_EPILOGUE + KI + j)
            ln_stats(NCH - 1, PX_EPILOGUE + KI + 1)
            ln_apply(NCH - 1)


def experts(nc, A, out, xkeep, ident):
    with ExitStack() as ctx:
        def sb(name, shape, dt=F32):
            return ctx.enter_context(nc.sbuf_tensor(name, shape, dt))

        def sem(name):
            return ctx.enter_context(nc.semaphore(name))

        xT = sb("x1T", [P, KD, L])
        w_r = sb("w_r", [P, KD, E])
        bias = sb("bias", [P, E])
        lg = sb("lg", [P, NT, E])
        corr = sb("corr", [P, NT, E + 2])
        zap = sb("zap", [P, NT, E + 2])
        top = sb("top", [P, NT, 8])
        rs = sb("rs", [P, NT])
        comb = sb("comb", [P, NT, EX])
        wgu = sb("wgu", [P, 2, KD, 2 * EI])
        wd = sb("wd", [P, 2, D])
        sg = sb("sg", [P, 2, CH])
        hm = sb("hm", [P, 2, CH])
        stats = sb("stats2", [P, NT, 6])
        mv = sb("mv2", [P, NT, 2])
        var = sb("var2", [P, NT])
        half = sb("half2", [P, NT])
        rstd = sb("rstd2", [P, NT])
        gu_ps = ctx.enter_context(nc.psum_tensor("gu_ps", [P, 2, 2, CH], F32))
        dn_ps = ctx.enter_context(nc.psum_tensor("dn_ps", [P, 2, TS, D], F32))

        s_w = sem("router_landed")
        s_e = [sem(f"expert_landed{i}") for i in range(2)]
        tr_full = sem("tr_full")
        tr_free = sem("tr_free")
        lg_full = sem("lg_full")
        route = sem("route_step")
        exp_done = sem("route_exp_done")
        comb_done = sem("comb_done")
        gu_full = sem("gu_full")
        sg_done = sem("sg_done")
        hm_done = sem("hm_done")
        dn_full = sem("dn_full")
        acc_done = sem("acc_done")
        ln_step = sem("ln2_step")
        var_done = sem("var2_done")
        rstd_done = sem("rstd2_done")
        y_done = sem("y_done")
        s_out = sem("out_written")
        NEVER = -3.0e38
        ZAPPED = -3.2e38

        block = ctx.enter_context(nc.Block())

        @block.sync
        def _(sp):
            sp.dma_start(w_r[:], A["router_T"].rearrange("(k p) e -> p k e", p=P)).then_inc(s_w, 16)
            sp.dma_start(bias[:], A["router_bias"].partition_broadcast(P)).then_inc(s_w, 16)
            gu_d = A["guT"].rearrange("e (k p) n -> e p k n", p=P)

            def load(e, slot, n):
                wait(sp, dn_full, NCH * (e - 1))
                sp.dma_start(wgu[:, slot], gu_d[bass.ds(e, 1)].rearrange("a p k n -> p (a k) n")).then_inc(s_e[slot], 16)
                sp.dma_start(wd[:, slot], A["dT"][bass.ds(e, 1)].rearrange("a p n -> p (a n)")).then_inc(s_e[slot], 16)

            load(0, 0, 0)
            load(1, 1, 0)
            with sp.Fori(1, EX // 2) as i:
                load(2 * i, 0, 0)
                load(2 * i + 1, 1, 0)
            o_d = out.rearrange("(j p) d -> p j d", p=P)
            for j in range(0, NT, TS):
                sp.wait_ge(y_done, j + TS)
                sp.dma_start(o_d[:, j:j + TS, :], xkeep[:, j:j + TS, :]).then_inc(s_out, 16)
            sp.wait_ge(s_out, 16 * (NT // TS))

        @block.tensor
        def _(pe):
            for b in range(KD * NCH):
                c, k = b // KD, b % KD
                wait(pe, tr_free, b - 3)
                for t in range(TS):
                    mm = pe.transpose(gu_ps[:, b % 4 // 2, b % 2, t * P:(t + 1) * P],
                                      xkeep[:, c * TS + t, k * P:(k + 1) * P], ident[:])
                mm.then_inc(tr_full, 1)
            pe.wait_ge(tr_free, KD * NCH)
            pe.wait_ge(s_w, 32)
            lg_ps = dn_ps[:].rearrange("p a t d -> p (a t d)")
            for j in range(NT):
                for k in range(KD):
                    mm = pe.matmul(lg_ps[:, j * E:(j + 1) * E], xT[:, k, j * P:(j + 1) * P], w_r[:, k, :],
                                   start=(k == 0), stop=(k == KD - 1))
            mm.then_inc(lg_full, 1)

            def gate_up(s, e, slot, c):
                if c == 0:
                    pe.wait_ge(s_e[slot], (e - slot) * 16 + 32)
                wait(pe, hm_done, s - 1)
                for half in range(2):
                    for k in range(KD):
                        mm = pe.matmul(gu_ps[:, c % 2, half, :], wgu[:, slot, k, half * EI:(half + 1) * EI],
                                       xT[:, k, c * CH:(c + 1) * CH], start=(k == 0), stop=(k == KD - 1))
                    mm.then_inc(gu_full, 1)

            def down(s, slot, c):
                pe.wait_ge(hm_done, s + 1)
                wait(pe, acc_done, TS * (s - 1))
                if c < 2:
                    pe.wait_ge(comb_done, 1)
                for t in range(TS):
                    mm = pe.matmul(dn_ps[:, c % 2, t, :], hm[:, c % 2, t * P:(t + 1) * P], wd[:, slot, :],
                                   start=True, stop=True)
                mm.then_inc(dn_full, 1)

            def pair(e, first):
                for j in range(2 * NCH):
                    s = NCH * e + j
                    gate_up(s, e + j // NCH, j // NCH, j % NCH)
                    if j > 0 or not first:
                        down(s - 1, (j - 1) // NCH % 2, (j - 1) % NCH)

            pair(0, True)
            with pe.Fori(1, EX // 2) as i:
                pair(2 * i, False)
            down(EX * NCH - 1, 1, NCH - 1)

        @block.scalar
        def _(act):
            for b in range(0, KD * NCH, 2):
                act.wait_ge(tr_full, b + 2)
                c = b // KD
                act.activation(xT[:, :, c * CH:(c + 1) * CH], gu_ps[:, b % 4 // 2, :, :],
                               ACT.Copy).then_inc(tr_free, 2)
            act.wait_ge(route, 2)
            act.activation(lg[:], lg[:], ACT.Exp).then_inc(exp_done, 1)

            def silu(s, c):
                act.wait_ge(gu_full, 2 * s + 1)
                wait(act, hm_done, s - 1)
                act.activation(sg[:, c % 2, :], gu_ps[:, c % 2, 0, :], ACT.Silu).then_inc(sg_done, 1)

            def pair(e):
                for j in range(2 * NCH):
                    silu(NCH * e + j, j % NCH)

            pair(0)
            with act.Fori(1, EX // 2) as i:
                pair(2 * i)

        @block.gpsimd
        def _(pool):
            pool.wait_ge(var_done, 1)
            pool.tensor_tensor(rstd[:], var[:], half[:], ALU.pow).then_inc(rstd_done, 1)

        @block.vector
        def _(ve):
            n = [0]

            def then(ins):
                n[0] += 1
                ins.then_inc(route, 1)
                ve.wait_ge(route, n[0])

            def rows(a):
                return a.unsqueeze(2).to_broadcast([P, NT, E])

            ve.wait_ge(lg_full, 1)
            ve.wait_ge(s_w, 32)
            lg_ps = dn_ps[:].rearrange("p a t d -> p (a t d)").rearrange("p (j e) -> p j e", e=E)
            then(ve.tensor_reduce(rs[:], lg_ps[:, 0:NT, :], AX.X, ALU.max))
            then(ve.tensor_tensor(lg[:], lg_ps[:, 0:NT, :], rows(rs[:]), ALU.subtract))
            ve.wait_ge(exp_done, 1)
            then(ve.tensor_reduce(rs[:], lg[:], AX.X, ALU.add))
            then(ve.reciprocal(rs[:], rs[:]))
            then(ve.tensor_tensor(lg[:], lg[:], rows(rs[:]), ALU.mult))
            ve.memset(corr[:, :, E:], NEVER)
            ve.memset(comb[:, :, E:], 1.0)
            then(ve.tensor_tensor(corr[:, :, 0:E], lg[:], bias[:].unsqueeze(1).to_broadcast([P, NT, E]), ALU.add))
            for j in range(NT):
                last = ve.max(top[:, j, :], corr[:, j, 0:E])
            then(last)
            then(ve.memset(top[:, :, TOPK:], NEVER))
            for j in range(NT):
                last = ve.match_replace(zap[:, j, :], top[:, j, :], corr[:, j, :], ZAPPED)
            then(last)
            then(ve.tensor_tensor(zap[:, :, 0:E], zap[:, :, 0:E], corr[:, :, 0:E], ALU.not_equal))
            then(ve.tensor_tensor(lg[:], lg[:], zap[:, :, 0:E], ALU.mult))
            then(ve.tensor_reduce(rs[:], lg[:], AX.X, ALU.add))
            then(ve.tensor_scalar(rs[:], rs[:], NORM_MIN, None, ALU.max))
            then(ve.reciprocal(rs[:], rs[:]))
            ve.tensor_tensor(comb[:, :, 0:E], lg[:], rows(rs[:]), ALU.mult).then_inc(comb_done, 1)
            ve.wait_ge(comb_done, 1)

            def product(s, c):
                ve.wait_ge(sg_done, s + 1)
                ve.wait_ge(gu_full, 2 * s + 2)
                wait(ve, dn_full, s - 1)
                ve.tensor_tensor(hm[:, c % 2, :], sg[:, c % 2, :], gu_ps[:, c % 2, 1, :], ALU.mult).then_inc(hm_done, 1)

            def accumulate(s, e, c):
                ve.wait_ge(dn_full, s + 1)
                for t in range(TS):
                    j = c * TS + t
                    w = comb[:, j, bass.ds(e, 1)]
                    ve.scalar_tensor_tensor(xkeep[:, j, :], dn_ps[:, c % 2, t, :], w, xkeep[:, j, :],
                                            ALU.mult, ALU.add).then_inc(acc_done, 1)

            def pair(e, first):
                for j in range(2 * NCH):
                    s = NCH * e + j
                    product(s, j % NCH)
                    if j > 0:
                        accumulate(s - 1, e + (j - 1) // NCH, (j - 1) % NCH)
                    elif not first:
                        accumulate(s - 1, e - 1, NCH - 1)

            pair(0, True)
            with ve.Fori(1, EX // 2) as i:
                pair(2 * i, False)
            accumulate(EX * NCH - 1, EX - 1, NCH - 1)

            ve.wait_ge(acc_done, EX * NT)
            for j in range(NT):
                ve.bn_stats(stats[:, j, :], xkeep[:, j, :]).then_inc(ln_step, 1)
            for j in range(NT):
                ve.wait_ge(ln_step, j + 1)
                ve.bn_aggr(mv[:, j, :], stats[:, j, :]).then_inc(ln_step, 1)
            ve.wait_ge(ln_step, 2 * NT)
            ve.memset(half[:], -0.5)
            ve.tensor_scalar(var[:], mv[:, :, 1], LN_EPS, None, ALU.add).then_inc(var_done, 1)
            ve.wait_ge(rstd_done, 1)
            for j in range(NT):
                ve.tensor_scalar(xkeep[:, j, :], xkeep[:, j, :], mv[:, j, 0:1], rstd[:, j:j + 1],
                                 ALU.subtract, ALU.mult).then_inc(y_done, 1)


def build(nc, A, out):
    with nc.sbuf_tensor("xkeep", [P, NT, D], F32) as xkeep, nc.sbuf_tensor("identity", [P, P], F32) as ident:
        mamba(nc, A, xkeep, ident)
        experts(nc, A, out, xkeep, ident)


def kernel(**inputs):
    import numpy as np
    import concourse.bacc as bacc
    from concourse.bass_utils import run_bass_kernel_spmd

    def T(a):
        return np.swapaxes(np.asarray(a), -1, -2)

    w = {k.replace("L0_attn_", "").replace("L0_ffn_", ""): np.asarray(v) for k, v in inputs.items()}
    x = w["x"].reshape(L, D)
    gu = np.concatenate([w["gate_up_proj"],
                         np.concatenate([w["shared_gate_w"].reshape(2, EI, D), w["shared_up_w"].reshape(2, EI, D)], 1)])
    down = np.concatenate([T(w["down_proj"]), T(w["shared_down_w"]).reshape(2, EI, D)])
    arrays = {
        "x": x, "xT": T(x), "W_inT": T(w["W_in"]), "W_dtT": T(w["W_dt"]), "W_outT": T(w["W_out"]),
        "W_BC3T": T(np.concatenate([w["W_B"], w["W_C"]] * 3)), "W_conv": w["W_conv"].reshape(DI, TAPS),
        "b_conv": w["b_conv"].reshape(KI, P).T, "b_dt": w["b_dt"].reshape(KI, P).T, "A_log": w["A_log"],
        "router_T": T(w["router_weight"]), "router_bias": w["e_score_bias"],
        "guT": T(gu), "dT": down,
        "ident": np.eye(P, dtype=np.float32), "sel3": np.tile(np.eye(BC, dtype=np.float32), (3, 1)),
    }
    arrays = {k: np.ascontiguousarray(v) for k, v in arrays.items()}
    nc = bacc.Bacc("TRN2", target_bir_lowering=False, num_devices=1)
    A = {k: nc.dram_tensor(k + "_d", v.shape, F32, kind="ExternalInput").ap() for k, v in arrays.items()}
    out = nc.dram_tensor("out_d", (L, D), F32, kind="ExternalOutput").ap()
    build(nc, A, out)
    r = run_bass_kernel_spmd(nc, [{k + "_d": v for k, v in arrays.items()}], core_ids=[0])
    return np.asarray(r.results[0]["out_d"]).reshape(1, L, D)
```

```python
from contextlib import ExitStack

import concourse.bass as bass
from concourse import mybir

F32 = mybir.dt.float32
BF16 = mybir.dt.bfloat16
ALU = mybir.AluOpType
ACT = mybir.ActivationFunctionType
AX = mybir.AxisListType

P = 128
D = 256
DI = 512
NST = 16
TAPS = 4
L = 4096
CH = 512
NCH = L // CH
KD = D // P
KI = DI // P
TS = CH // P
NT = L // P
E = 32
EI = 128
TOPK = 6
EX = E + 2
LN_EPS = 1e-5
NORM_MIN = 1e-12
BC = 2 * NST

SW = 2 * NST
MH = KI // 2
HD = DI // 2

PE_STEPS = {
    0: [("IN", 0)], 1: [("IN", 1)], 2: [("IN", 2)], 3: [("IN", 3)],
    4: [("Z", 0)], 5: [("Z", 1)], 6: [("Z", 2)], 7: [("Z", 3)],
    9: [("GT", 0), ("GT", 1)], 10: [("GT", 2), ("GT", 3)],
    11: [("BC", 0)], 13: [("DT", 0)], 15: [("DT", 1)], 17: [("DT", 2)], 19: [("DT", 3)],
    21: [("OUT", 0)], 23: [("OUT", 1)],
}
LONG = {"BC", "DT", "OUT"}
AHEAD = {"IN", "BC", "DT"}
BEHIND = {"GT", "OUT"}
ACT_STEPS = {
    2: [("IN", 0)], 3: [("IN", 1)], 4: [("IN", 2)], 5: [("IN", 3)],
    6: [("Z", 0)], 7: [("Z", 1)], 8: [("Z", 2)], 9: [("Z", 3), ("TANH", 0)],
    10: [("TANH", 1), ("TANH", 2)], 11: [("TANH", 3), ("GT", 0)], 12: [("GT", 1), ("GT", 2)], 13: [("GT", 3)],
    14: [("BC", 0)], 16: [("DT", 0)], 17: [("ABS", 0)], 18: [("DT", 1), ("EXP", 0)], 19: [("ABS", 1)],
    20: [("DT", 2), ("EXP", 1)], 21: [("ABS", 2)], 22: [("DT", 3), ("EXP", 2)], 23: [("ABS", 3)],
    24: [("EXP", 3)], 25: [("LN", 0)], 26: [("LN", 1)], 27: [("LN", 2)], 28: [("LN", 3)],
}
VE_STEPS = {
    1: [("GATE", 1)],
    6: [("CONV", 0), ("CONV", 1)], 7: [("Z", 0), ("CONV", 2), ("CONV", 3)], 8: [("Z", 1)], 9: [("Z", 2)],
    10: [("Z", 3)], 11: [("SILU", 0), ("SILU", 1)], 12: [("SILU", 2), ("SILU", 3)],
    15: [("BC", 0)], 17: [("GATE", 0)], 24: [("OUT", 0)], 26: [("OUT", 1), ("STATS", 0)],
    27: [("SOFT", 0)], 28: [("SOFT", 1)], 29: [("SOFT", 2)], 30: [("SOFT", 3), ("NORM", 0)],
}
AHEAD_TOO = AHEAD | {"TANH", "ABS", "EXP", "LN", "CONV", "SILU", "SOFT"}
BEHIND_TOO = BEHIND | {"STATS", "NORM"}
PROLOGUE = [("IN", m) for m in range(KI)] + [("BC", 0)] + [("DT", m) for m in range(KI)]
EPILOGUE = [("GT", m) for m in range(KI)] + [("OUT", 0), ("OUT", 1)]


def bank(use):
    return (use[1] + (use[0] == "DT")) % 2


def tasks(steps, s, ahead, behind):
    return [u for u in steps.get(s, [])
            if (ahead or u[0] not in AHEAD_TOO) and (behind or u[0] not in BEHIND_TOO)]


def body_uses(b, ahead, behind):
    return [u for s in range(SW) for u in tasks(PE_STEPS, s, ahead, behind) if bank(u) == b]


def px_base(b, c):
    base = len([u for u in PROLOGUE if bank(u) == b])
    if isinstance(c, int) and c == 0:
        return base
    return base + len(body_uses(b, True, False)) + (c - 1) * len(body_uses(b, True, True))


def use_no(u, c, ahead, behind):
    b = bank(u)
    if isinstance(c, str) and c == "prologue":
        return [v for v in PROLOGUE if bank(v) == b].index(u)
    if isinstance(c, str) and c == "epilogue":
        before = px_base(b, NCH - 1) + len(body_uses(b, False, True))
        return before + [v for v in EPILOGUE if bank(v) == b].index(u)
    return px_base(b, c) + body_uses(b, ahead, behind).index(u)


def wait(eng, sem, value):
    if isinstance(value, int) and value <= 0:
        return
    eng.wait_ge(sem, value)


def chunks(eng, body):
    body(0, 0, True, False)
    with eng.Fori(0, (NCH - 2) // 2) as i:
        body(2 * i + 1, 1, True, True)
        body(2 * i + 2, 0, True, True)
    body(NCH - 1, 1, False, True)


def mamba(nc, A, xkeep, ident):
    with ExitStack() as ctx:
        def sb(name, shape, dt=F32):
            return ctx.enter_context(nc.sbuf_tensor(name, shape, dt))

        def sem(name):
            return ctx.enter_context(nc.semaphore(name))

        w_in = sb("w_in", [P, KD, 2 * DI])
        w_dt = sb("w_dt", [P, KI, DI])
        w_bc = sb("w_bc", [P, KI, 3 * BC])
        w_out = sb("w_out", [P, KI, D])
        w_conv = sb("w_conv", [P, KI, TAPS])
        b_conv = sb("b_conv", [P, KI])
        b_dt = sb("b_dt", [P, KI])
        a_neg = sb("a_neg", [P, KI, NST])
        sel_f = sb("sel_f", [3 * BC, BC])
        sel = sb("sel", [3 * BC, BC], BF16)
        xT = sb("xT", [P, 2, KD, CH])
        xr = sb("xr", [P, TS, D])
        xin = sb("xin", [P, KI, TAPS - 1 + CH])
        u_sb = sb("u", [P, KI, CH])
        scr = sb("scr", [P, KI, CH])
        vb = sb("vb", [P, KI, CH])
        g = sb("g", [P, TS, DI])
        gT = sb("gT", [P, KI, CH])
        dt = sb("dt", [P, 2, KI, CH])
        dtu = sb("dtu", [P, KI, CH])
        dbu = sb("dbu", [P, 2, MH, CH])
        h = sb("h", [P, 2, MH, CH])
        hc = sb("hc", [P, 2, MH, CH])
        zg = sb("zg", [P, TS, DI])
        thz = scr[:, KI - 1, :]
        bb = sb("bb", [P, NST, CH])
        brow = scr[0:NST, 1, :]
        bc3 = sb("bc3", [3 * BC, 2, CH], BF16)
        bcr = scr[0:3 * BC, 0, :]
        b_dram = nc.dram_tensor("b_rows", (2, NST, CH), F32, kind="Internal").ap()
        carry = sb("carry", [P, NST, KI])
        stats = sb("stats", [P, TS, 6])
        mv = sb("mv", [P, TS, 2])
        var = sb("var", [P, TS])
        half_c = sb("half", [P, TS])
        rstd = sb("rstd", [P, TS])
        y_ps = ctx.enter_context(nc.psum_tensor("y_ps", [P, TS, HD], F32))
        da_ps = ctx.enter_context(nc.psum_tensor("da_ps", [P, 2, CH], F32))
        cb_ps = ctx.enter_context(nc.psum_tensor("cb_ps", [P, 2, CH], F32))
        px = ctx.enter_context(nc.psum_tensor("px", [P, 2, CH], F32))

        s_w = sem("weights_landed")
        s_xT = [sem(f"xT_landed{i}") for i in range(2)]
        s_xr = sem("xr_landed")
        px_full = [sem(f"px_full{i}") for i in range(2)]
        px_free = [sem(f"px_free{i}") for i in range(2)]
        brow_done = sem("brow_done")
        brow_stored = sem("brow_stored")
        bb_landed = [sem(f"bb_landed{i}") for i in range(NST)]
        prep = sem("prep_act")
        prepv = sem("prep_vector")
        conv_step = sem("conv_step")
        head_done = sem("head_done")
        tanh_u = sem("tanh_u_done")
        u_done = sem("u_done")
        bc_hi = sem("bc_hi_done")
        bc_step = sem("bc_step")
        soft_abs = sem("soft_abs_done")
        soft_exp = sem("soft_exp_done")
        soft_log = sem("soft_log_done")
        dt_done = sem("dt_done")
        dtu_done = sem("dtu_done")
        dbu_done = sem("dbu_done")
        da_full = sem("da_full")
        scan_done = sem("scan_done")
        carry_done = sem("carry_done")
        cb_full = sem("cb_full")
        hc_done = sem("hc_done")
        ytr_done = sem("ytr_done")
        tanh_z = sem("tanh_z_done")
        g_done = sem("g_done")
        ln_step = sem("ln_step")
        stats_seen = sem("stats_seen")
        var_done = sem("var_done")
        rstd_done = sem("rstd_done")
        x1_done = sem("x1_done")

        block = ctx.enter_context(nc.Block())
        NW = 10

        @block.sync
        def _(sp):
            for dst, src in (
                (w_in[:], A["W_inT"].rearrange("(k p) n -> p k n", p=P)),
                (w_conv[:], A["W_conv"].rearrange("(m p) t -> p m t", p=P)),
                (b_conv[:], A["b_conv"]),
                (b_dt[:], A["b_dt"]),
                (w_bc[:], A["W_BC3T"].rearrange("(k p) n -> p k n", p=P)),
                (a_neg[:], A["A_log"].rearrange("(m p) s -> p m s", p=P)),
                (w_dt[:], A["W_dtT"].rearrange("(k p) n -> p k n", p=P)),
                (sel_f[:], A["sel3"]),
                (ident[:], A["ident"]),
                (w_out[:], A["W_outT"].rearrange("(k p) n -> p k n", p=P)),
            ):
                sp.dma_start(dst, src).then_inc(s_w, 16)
            xT_d = A["xT"].rearrange("(k p) t -> p k t", p=P)
            x_d = A["x"].rearrange("(j p) d -> p j d", p=P)
            sp.dma_start(xT[:, 0], xT_d[:, :, 0:CH]).then_inc(s_xT[0], 16)

            def load_rows(o):
                wait(sp, x1_done, TS * o)
                sp.dma_start(xr[:], x_d[:, bass.ds(o * TS, TS), :]).then_inc(s_xr, 16)

            def spread_rows(q, qpar):
                sp.wait_ge(brow_done, q + 1)
                sp.dma_start(b_dram[qpar], brow[:]).then_inc(brow_stored, 16)
                sp.wait_ge(brow_stored, 16 * (q + 1))
                for n in range(NST):
                    wait(sp, dbu_done, SW * q - NST + n + 1)
                    sp.dma_start(bb[:, n, :], b_dram[qpar, n].partition_broadcast(P)).then_inc(bb_landed[n], 16)

            def load_xT(q, qpar):
                wait(sp, tanh_z, TS * (q - 1))
                sp.dma_start(xT[:, qpar], xT_d[:, :, bass.ds(q * CH, CH)]).then_inc(s_xT[qpar], 16)

            def body(c, par):
                if not (isinstance(c, int) and c == 0):
                    load_rows(c - 1)
                if not (isinstance(c, int) and c + 2 >= NCH):
                    load_xT(c + 2, par)
                spread_rows(c + 1, 1 - par)

            load_xT(1, 1)
            spread_rows(0, 0)
            body(0, 0)
            with sp.Fori(0, (NCH - 4) // 2) as i:
                body(2 * i + 1, 1)
                body(2 * i + 2, 0)
            body(NCH - 3, 1)
            body(NCH - 2, 0)
            load_rows(NCH - 2)
            load_rows(NCH - 1)
            sp.wait_ge(x1_done, TS * NCH)

        @block.tensor
        def _(pe):
            def part(u, k0, k1, q, qpar, i, before=None):
                kind, m = u
                b = bank(u)
                out = px[:, b, :]
                last = k1 == (KD if kind in ("IN", "Z") else KI)
                if k0 == 0:
                    if kind == "IN" and m == 0:
                        pe.wait_ge(s_xT[qpar], (q - qpar) * 8 + 16)
                    if kind == "BC":
                        pe.wait_ge(u_done, KI * (q + 1))
                    if kind == "GT" and m == 0:
                        pe.wait_ge(g_done, 2 * TS * (q + 1))
                    if kind == "OUT" and m == 0:
                        for v in (KI - 2, KI - 1):
                            pe.wait_ge(px_free[bank(("GT", v))], before[v - KI + 2] + 1)
                    wait(pe, px_free[b], i)
                if kind == "GT":
                    for t in range(TS):
                        mm = pe.transpose(px[:, b, t * P:(t + 1) * P], g[:, t, m * P:(m + 1) * P], ident[:])
                    mm.then_inc(px_full[b], 1)
                    return
                for t in range(2 if kind == "OUT" else 1):
                    for k in range(k0, k1):
                        if kind == "IN":
                            lhsT, rhs = w_in[:, k, m * P:(m + 1) * P], xT[:, qpar, k, :]
                        elif kind == "Z":
                            lhsT, rhs = xT[:, qpar, k, m * P:(m + 1) * P], w_in[:, k, DI:2 * DI]
                        elif kind == "BC":
                            lhsT, rhs, out = w_bc[:, k, :], u_sb[:, k, :], px[0:3 * BC, b, :]
                        elif kind == "DT":
                            lhsT, rhs = w_dt[:, k, m * P:(m + 1) * P], u_sb[:, k, :]
                        else:
                            ts = 2 * m + t
                            lhsT, rhs = gT[:, k, ts * P:(ts + 1) * P], w_out[:, k, :]
                            out = px[:, b, t * D:(t + 1) * D]
                        mm = pe.matmul(out, lhsT, rhs, start=(k == 0 and t == 0), stop=(k == k1 - 1 and last),
                                       skip_group_check=(kind == "OUT"))
                if last:
                    mm.then_inc(px_full[b], 1)

            def spread_c(c, s, par):
                n = s % NST
                if s == 0:
                    pe.wait_ge(bc_step, 3 * (c + 1))
                wait(pe, hc_done, SW * c + s - 1)
                pe.matmul(cb_ps[:, s % 2, :], sel[:, NST + n:NST + n + 1].to_broadcast([3 * BC, P]), bc3[:, par, :],
                          start=True, stop=True).then_inc(cb_full, 1)

            def sum_states(c, s):
                pe.wait_ge(hc_done, SW * c + s + 1)
                if s % NST == 0:
                    wait(pe, g_done, TS * (2 * c + s // NST))
                for t in range(TS):
                    for m in range(MH):
                        mm = pe.matmul(y_ps[:, t, m * P:(m + 1) * P], hc[:, s % 2, m, t * P:(t + 1) * P],
                                       ident[:], is_transpose=True, start=(s % NST == 0 and m == 0 and t % 2 == 0),
                                       stop=(s % NST == NST - 1 and m == MH - 1 and t % 2 == 1), skip_group_check=True)
                mm.then_inc(ytr_done, 1)

            def whole(u, q, qpar, c):
                i = use_no(u, c, False, False)
                before = [use_no(("GT", v), c, False, False) for v in (KI - 2, KI - 1)] if u[0] == "OUT" else None
                part(u, 0, KI if u[0] in LONG else KD, q, qpar, i, before)

            pe.wait_ge(s_w, 16 * NW)
            pe.wait_ge(prepv, 3)
            for u in PROLOGUE:
                whole(u, 0, 0, "prologue")
            spread_c(0, 0, 0)

            def body(c, par, ahead, behind):
                for s in range(SW):
                    if s + 1 < SW:
                        spread_c(c, s + 1, par)
                    elif ahead:
                        spread_c(c + 1, 0, 1 - par)
                    if s > 0:
                        sum_states(c, s - 1)
                    elif behind:
                        sum_states(c - 1, SW - 1)
                    for first, at in ((False, s - 1), (True, s)):
                        for u in tasks(PE_STEPS, at, ahead, behind):
                            if not first and u[0] not in LONG:
                                continue
                            q, qpar = ((c + 1, 1 - par) if u[0] in AHEAD else (c - 1, 1 - par) if u[0] in BEHIND
                                       else (c, par))
                            i = use_no(u, c, ahead, behind)
                            if u[0] not in LONG:
                                part(u, 0, KD, q, qpar, i)
                            elif u[0] == "OUT" and first:
                                before = [use_no(("GT", v), c, ahead, behind) for v in (KI - 2, KI - 1)]
                                part(u, 0, KI, q, qpar, i, before)
                            elif u[0] != "OUT":
                                part(u, 0 if first else KI // 2, KI // 2 if first else KI, q, qpar, i)

            chunks(pe, body)
            sum_states(NCH - 1, SW - 1)
            for u in EPILOGUE:
                whole(u, NCH - 1, 1, "epilogue")

        @block.scalar
        def _(act):
            def task(u, q, qpar, i, before=None):
                kind, m = u
                b = bank(u)
                if kind in ("IN", "Z", "GT", "BC", "DT"):
                    act.wait_ge(px_full[b], i + 1)
                if kind == "IN":
                    if m == 0:
                        act.wait_ge(head_done, q + 1)
                    act.activation(xin[:, m, TAPS - 1:], px[:, b, :], ACT.Copy).then_inc(px_free[b], 1)
                elif kind == "TANH":
                    act.wait_ge(conv_step, KI * TAPS * q + KI * (TAPS - 1) + m + 1)
                    if before is not None:
                        act.wait_ge(px_free[bank(("Z", TS - 1))], before + 1)
                    act.activation(scr[:, m, :], u_sb[:, m, :], ACT.Tanh).then_inc(tanh_u, 1)
                elif kind == "BC":
                    wait(act, brow_stored, 16 * q)
                    act.activation(brow[:], px[0:NST, b, :], ACT.Copy).then_inc(brow_done, 1)
                    act.activation(bc3[:, qpar, :], px[0:3 * BC, b, :], ACT.Copy).then_inc(bc_hi, 1)
                elif kind == "DT":
                    wait(act, dt_done, KI * q)
                    act.activation(vb[:, m, :], px[:, b, :], ACT.Identity, bias=b_dt[:, m:m + 1]).then_inc(px_free[b], 1)
                elif kind == "ABS":
                    act.wait_ge(px_free[bank(("DT", m))], i + 1)
                    act.wait_ge(bc_step, 3 * (q + 1))
                    act.wait_ge(brow_stored, 16 * (q + 1))
                    act.activation(scr[:, m, :], vb[:, m, :], ACT.Abs).then_inc(soft_abs, 1)
                elif kind == "EXP":
                    act.wait_ge(soft_abs, KI * q + m + 1)
                    act.activation(scr[:, m, :], scr[:, m, :], ACT.Exp, scale=-1.0).then_inc(soft_exp, 1)
                elif kind == "LN":
                    act.wait_ge(soft_exp, KI * q + m + 1)
                    act.activation(scr[:, m, :], scr[:, m, :], ACT.Ln, bias=1.0).then_inc(soft_log, 1)
                elif kind == "GT":
                    act.activation(gT[:, m, :], px[:, b, :], ACT.Copy).then_inc(px_free[b], 1)
                elif kind == "Z":
                    if m > 0:
                        act.wait_ge(px_free[1 - b], before + 1)
                    act.activation(thz[:], px[:, b, :], ACT.Tanh).then_inc(tanh_z, 1)

            def decay(c, par, s, m):
                n, mt = s % NST, s // NST * MH + m
                if n == 0 and m == 0:
                    act.wait_ge(dt_done, KI * c + mt + MH)
                wait(act, scan_done, (SW * c + s) * MH + m - 1)
                act.activation(da_ps[:, m, :], dt[:, par, mt, :], ACT.Exp,
                               scale=a_neg[:, mt, n:n + 1]).then_inc(da_full, 1)

            def keep_state(c, s):
                n, m0 = s % NST, s // NST * MH
                act.wait_ge(scan_done, (SW * c + s + 1) * MH)
                act.activation(carry[:, n, m0:m0 + MH], h[:, s % 2, :, CH - 1], ACT.Copy).then_inc(carry_done, 1)

            act.wait_ge(s_w, 16 * NW)
            act.activation(a_neg[:], a_neg[:], ACT.Exp).then_inc(prep, 1)
            act.wait_ge(prepv, 4)
            for kind in ("IN", "TANH", "BC", "DT", "ABS", "EXP", "LN"):
                for m in range(1 if kind == "BC" else KI):
                    of = ("DT", m) if kind == "ABS" else (kind, m)
                    task((kind, m), 0, 0, use_no(of, "prologue", 0, 0) if of in PROLOGUE else None)

            def body(c, par, ahead, behind):
                for s in range(SW):
                    decay(c, par, s, 0)
                    if s > 0:
                        keep_state(c, s - 1)
                    elif behind:
                        keep_state(c - 1, SW - 1)
                    decay(c, par, s, 1)
                    for u in tasks(ACT_STEPS, s, ahead, behind):
                        q, qpar = ((c + 1, 1 - par) if u[0] in AHEAD_TOO else (c - 1, 1 - par) if u[0] in BEHIND_TOO
                                   else (c, par))
                        of = ("DT", u[1]) if u[0] == "ABS" else u
                        i = use_no(of, c, ahead, behind) if of[0] in ("IN", "Z", "GT", "BC", "DT") else None
                        before = use_no(("Z", u[1] - 1), c, ahead, behind) if u[0] == "Z" and u[1] > 0 else None
                        if u == ("TANH", KI - 1):
                            before = use_no(("Z", TS - 1), c, ahead, behind)
                        task(u, q, qpar, i, before)

            chunks(act, body)
            for m in range(KI):
                task(("GT", m), NCH - 1, 1, use_no(("GT", m), "epilogue", 0, 0))

        @block.gpsimd
        def _(pool):
            def times_u(q, qpar, half):
                pool.wait_ge(dt_done, KI * q + MH * (half + 1))
                wait(pool, dbu_done, SW * (q - 1) + NST * (half + 1))
                r = slice(MH * half, MH * (half + 1))
                pool.tensor_tensor(dtu[:, r, :], dt[:, qpar, r, :], u_sb[:, r, :], ALU.mult).then_inc(dtu_done, 1)

            def times_b(c, s):
                n, half = s % NST, s // NST
                if n == 0:
                    pool.wait_ge(dtu_done, 2 * c + half + 1)
                if half == 0:
                    pool.wait_ge(bb_landed[n], 16 * (c + 1))
                wait(pool, scan_done, MH * (SW * c + s - 1))
                pool.tensor_tensor(dbu[:, s % 2], dtu[:, MH * half:MH * (half + 1), :],
                                   bb[:, n, :].unsqueeze(1).to_broadcast([P, MH, CH]), ALU.mult).then_inc(dbu_done, 1)

            def ln_rstd(o):
                pool.wait_ge(var_done, o + 1)
                pool.tensor_tensor(rstd[:], var[:], half_c[:], ALU.pow).then_inc(rstd_done, 1)

            times_u(0, 0, 0)

            def body(c, par, ahead, behind):
                for s in range(SW):
                    times_b(c, s)
                    if s == 1:
                        times_u(c, par, 1)
                    if behind and s == SW - 3:
                        ln_rstd(c - 1)
                if ahead:
                    times_u(c + 1, 1 - par, 0)

            chunks(pool, body)
            ln_rstd(NCH - 1)

        @block.vector
        def _(ve):
            def task(u, q, qpar, i):
                kind, m = u
                b = bank(u)
                if kind == "CONV":
                    conv_tap(q, m, i)
                elif kind == "SILU":
                    ve.wait_ge(tanh_u, KI * q + m + 1)
                    ve.scalar_tensor_tensor(u_sb[:, m, :], scr[:, m, :], 1.0, u_sb[:, m, :],
                                            ALU.add, ALU.mult).then_inc(u_done, 1)
                elif kind == "BC":
                    bc_parts(q, qpar, b, i)
                elif kind == "SOFT":
                    ve.wait_ge(soft_log, KI * q + m + 1)
                    ve.scalar_tensor_tensor(dt[:, qpar, m, :], vb[:, m, :], 0.0, scr[:, m, :],
                                            ALU.max, ALU.add).then_inc(dt_done, 1)
                elif kind == "GATE":
                    ve.wait_ge(ytr_done, SW * q + NST * (m + 1))
                    for t in range(TS):
                        ve.tensor_tensor(g[:, t, m * HD:(m + 1) * HD], y_ps[:, t, :], zg[:, t, m * HD:(m + 1) * HD],
                                         ALU.mult).then_inc(g_done, 1)
                elif kind == "Z":
                    ve.wait_ge(tanh_z, TS * q + m + 1)
                    ve.scalar_tensor_tensor(zg[:, m, :], thz[:], 1.0, px[:, b, :], ALU.add, ALU.mult).then_inc(px_free[b], 1)
                elif kind == "OUT":
                    ve.wait_ge(px_full[b], i + 1)
                    ve.wait_ge(s_xr, 16 * (q + 1))
                    r = xr[:, 2 * m:2 * m + 2, :]
                    ve.tensor_tensor(r, px[:, b, :].rearrange("p (t d) -> p t d", t=2), r, ALU.add).then_inc(px_free[b], 1)
                elif kind == "STATS":
                    ln_stats(q, i)
                elif kind == "NORM":
                    ve.wait_ge(rstd_done, q + 1)
                    for t in range(TS):
                        ve.tensor_scalar(xkeep[:, bass.ds(q * TS + t, 1), :], xr[:, t:t + 1, :], mv[:, t, 0:1],
                                         rstd[:, t:t + 1], ALU.subtract, ALU.mult).then_inc(x1_done, 1)

            def conv_tap(q, k, i):
                for m in range(KI):
                    src = xin[:, m, k:k + CH]
                    if k == 0:
                        if m == 0:
                            for v in (2, 3):
                                ve.wait_ge(px_free[bank(("IN", v))], i[v - 2] + 1)
                            wait(ve, dtu_done, 2 * q)
                        ve.tensor_scalar(u_sb[:, m, :], src, w_conv[:, m, 0:1], b_conv[:, m:m + 1],
                                         ALU.mult, ALU.add).then_inc(conv_step, 1)
                    else:
                        ve.wait_ge(conv_step, KI * TAPS * q + KI * (k - 1) + m + 1)
                        ve.scalar_tensor_tensor(u_sb[:, m, :], src, w_conv[:, m, k:k + 1], u_sb[:, m, :],
                                                ALU.mult, ALU.add).then_inc(conv_step, 1)
                if k == TAPS - 1:
                    ve.wait_ge(conv_step, KI * TAPS * (q + 1))
                    ve.tensor_copy(xin[:, :, 0:TAPS - 1], xin[:, :, CH:CH + TAPS - 1]).then_inc(head_done, 1)

            def bc_parts(q, par, b, i):
                lo, lo2 = slice(BC, 2 * BC), slice(2 * BC, 3 * BC)
                ve.wait_ge(bc_hi, q + 1)
                for r in (lo, lo2):
                    last = ve.tensor_tensor(bcr[r], px[r, b, :], bc3[r, par, :], ALU.subtract)
                last.then_inc(px_free[b], 1)
                ve.wait_ge(px_free[b], i + 1)
                for r in (lo, lo2):
                    last = ve.tensor_copy(bc3[r, par, :], bcr[r])
                last.then_inc(bc_step, 1)
                ve.wait_ge(bc_step, 3 * q + 1)
                ve.tensor_tensor(bcr[lo2], bcr[lo2], bc3[lo2, par, :], ALU.subtract).then_inc(bc_step, 1)
                ve.wait_ge(bc_step, 3 * q + 2)
                ve.tensor_copy(bc3[lo2, par, :], bcr[lo2]).then_inc(bc_step, 1)

            def ln_stats(o, i):
                for v in (0, 1):
                    ve.wait_ge(px_free[bank(("OUT", v))], i[v] + 1)
                for t in range(TS):
                    ve.bn_stats(stats[:, t, :], xr[:, t, :]).then_inc(ln_step, 1)
                ve.wait_ge(ln_step, 2 * TS * o + TS)
                ve.sem_inc(stats_seen, 1)
                for t in range(TS):
                    ve.bn_aggr(mv[:, t, :], stats[:, t, :]).then_inc(ln_step, 1)
                ve.wait_ge(ln_step, 2 * TS * (o + 1))
                ve.tensor_scalar(var[:], mv[:, :, 1], LN_EPS, None, ALU.add).then_inc(var_done, 1)

            def scans(c, s):
                n, m0 = s % NST, s // NST * MH
                ve.wait_ge(dbu_done, SW * c + s + 1)
                wait(ve, hc_done, SW * c + s - 1)
                wait(ve, carry_done, SW * c + s - 1)
                for m in range(MH):
                    ve.wait_ge(da_full, MH * (SW * c + s) + m + 1)
                    ve.tensor_tensor_scan(h[:, s % 2, m, :], da_ps[:, m, :], dbu[:, s % 2, m, :],
                                          carry[:, n, m0 + m:m0 + m + 1], ALU.mult, ALU.add).then_inc(scan_done, 1)

            def times_c(c, s):
                ve.wait_ge(cb_full, SW * c + s + 1)
                ve.wait_ge(scan_done, MH * (SW * c + s + 1))
                wait(ve, ytr_done, SW * c + s - 1)
                ve.tensor_tensor(hc[:, s % 2], h[:, s % 2],
                                 cb_ps[:, s % 2, :].unsqueeze(1).to_broadcast([P, MH, CH]),
                                 ALU.mult).then_inc(hc_done, 1)

            ve.memset(xin[:, :, 0:TAPS - 1], 0.0).then_inc(head_done, 1)
            ve.memset(carry[:], 0.0)
            ve.memset(half_c[:], -0.5)
            ve.wait_ge(s_w, 16 * NW)
            ve.tensor_copy(sel[:], sel_f[:]).then_inc(prepv, 1)
            ve.tensor_scalar(w_in[:, :, DI:], w_in[:, :, DI:], 0.5, None, ALU.mult).then_inc(prepv, 1)
            ve.tensor_scalar(w_conv[:], w_conv[:], 0.5, None, ALU.mult).then_inc(prepv, 1)
            ve.tensor_scalar(b_conv[:], b_conv[:], 0.5, None, ALU.mult)
            ve.wait_ge(prep, 1)
            ve.tensor_scalar(a_neg[:], a_neg[:], -1.0, None, ALU.mult).then_inc(prepv, 1)
            ve.wait_ge(prepv, 4)

            for kind in ("CONV", "SILU", "BC", "SOFT"):
                for m in range(1 if kind == "BC" else KI):
                    i = ([use_no(("IN", v), "prologue", 0, 0) for v in (2, 3)] if kind == "CONV" else
                         use_no(("BC", 0), "prologue", 0, 0) if kind == "BC" else None)
                    task((kind, m), 0, 0, i)

            def body(c, par, ahead, behind):
                for s in range(SW):
                    scans(c, s)
                    for u in tasks(VE_STEPS, s, ahead, behind):
                        kind, m = u
                        if kind == "GATE" and m == 1:
                            if behind:
                                task(u, c - 1, 1 - par, None)
                            continue
                        q, qpar = ((c + 1, 1 - par) if kind in AHEAD_TOO else (c - 1, 1 - par) if kind in BEHIND_TOO
                                   else (c, par))
                        i = None
                        if kind == "CONV":
                            i = [use_no(("IN", v), c, ahead, behind) for v in (2, 3)]
                        elif kind == "STATS":
                            i = [use_no(("OUT", v), c, ahead, behind) for v in (0, 1)]
                        elif kind in ("OUT", "BC"):
                            i = use_no(u, c, ahead, behind)
                        task(u, q, qpar, i)
                    if s > 0:
                        times_c(c, s - 1)
                    elif behind:
                        times_c(c - 1, SW - 1)

            chunks(ve, body)
            times_c(NCH - 1, SW - 1)
            task(("GATE", 1), NCH - 1, 1, None)
            for m in range(2):
                task(("OUT", m), NCH - 1, 1, use_no(("OUT", m), "epilogue", 0, 0))
            task(("STATS", 0), NCH - 1, 1, [use_no(("OUT", v), "epilogue", 0, 0) for v in (0, 1)])
            task(("NORM", 0), NCH - 1, 1, None)


def experts(nc, A, out, xkeep, ident):
    with ExitStack() as ctx:
        def sb(name, shape, dt=F32):
            return ctx.enter_context(nc.sbuf_tensor(name, shape, dt))

        def sem(name):
            return ctx.enter_context(nc.semaphore(name))

        xT = sb("x1T", [P, KD, L])
        w_r = sb("w_r", [P, KD, E])
        bias = sb("bias", [P, E])
        lg = sb("lg", [P, NT, E])
        corr = sb("corr", [P, NT, E + 2])
        zap = sb("zap", [P, NT, E + 2])
        top = sb("top", [P, NT, 8])
        rs = sb("rs", [P, NT])
        comb = sb("comb", [P, NT, EX])
        wgu = sb("wgu", [P, 2, KD, 2 * EI])
        wd = sb("wd", [P, 2, D])
        sg = sb("sg", [P, 2, CH])
        hm = sb("hm", [P, 2, CH])
        stats = sb("stats2", [P, NT, 6])
        mv = sb("mv2", [P, NT, 2])
        var = sb("var2", [P, NT])
        half = sb("half2", [P, NT])
        rstd = sb("rstd2", [P, NT])
        gu_ps = ctx.enter_context(nc.psum_tensor("gu_ps", [P, 2, 2, CH], F32))
        dn_ps = ctx.enter_context(nc.psum_tensor("dn_ps", [P, 2, TS, D], F32))

        s_w = sem("router_landed")
        s_e = [sem(f"expert_landed{i}") for i in range(2)]
        tr_full = sem("tr_full")
        tr_free = sem("tr_free")
        lg_full = sem("lg_full")
        route = sem("route_step")
        exp_done = sem("route_exp_done")
        comb_done = sem("comb_done")
        gu_full = sem("gu_full")
        sg_done = sem("sg_done")
        hm_done = sem("hm_done")
        dn_full = sem("dn_full")
        acc_done = sem("acc_done")
        ln_step = sem("ln2_step")
        var_done = sem("var2_done")
        rstd_done = sem("rstd2_done")
        y_done = sem("y_done")
        s_out = sem("out_written")
        NEVER = -3.0e38
        ZAPPED = -3.2e38

        block = ctx.enter_context(nc.Block())

        @block.sync
        def _(sp):
            sp.dma_start(w_r[:], A["router_T"].rearrange("(k p) e -> p k e", p=P)).then_inc(s_w, 16)
            sp.dma_start(bias[:], A["router_bias"].partition_broadcast(P)).then_inc(s_w, 16)
            gu_d = A["guT"].rearrange("e (k p) n -> e p k n", p=P)

            def load(e, slot, n):
                wait(sp, dn_full, NCH * (e - 1))
                sp.dma_start(wgu[:, slot], gu_d[bass.ds(e, 1)].rearrange("a p k n -> p (a k) n")).then_inc(s_e[slot], 16)
                sp.dma_start(wd[:, slot], A["dT"][bass.ds(e, 1)].rearrange("a p n -> p (a n)")).then_inc(s_e[slot], 16)

            load(0, 0, 0)
            load(1, 1, 0)
            with sp.Fori(1, EX // 2) as i:
                load(2 * i, 0, 0)
                load(2 * i + 1, 1, 0)
            o_d = out.rearrange("(j p) d -> p j d", p=P)
            for j in range(0, NT, TS):
                sp.wait_ge(y_done, j + TS)
                sp.dma_start(o_d[:, j:j + TS, :], xkeep[:, j:j + TS, :]).then_inc(s_out, 16)
            sp.wait_ge(s_out, 16 * (NT // TS))

        @block.tensor
        def _(pe):
            for b in range(KD * NCH):
                c, k = b // KD, b % KD
                wait(pe, tr_free, b - 3)
                for t in range(TS):
                    mm = pe.transpose(gu_ps[:, b % 4 // 2, b % 2, t * P:(t + 1) * P],
                                      xkeep[:, c * TS + t, k * P:(k + 1) * P], ident[:])
                mm.then_inc(tr_full, 1)
            pe.wait_ge(tr_free, KD * NCH)
            pe.wait_ge(s_w, 32)
            lg_ps = dn_ps[:].rearrange("p a t d -> p (a t d)")
            for j in range(NT):
                for k in range(KD):
                    mm = pe.matmul(lg_ps[:, j * E:(j + 1) * E], xT[:, k, j * P:(j + 1) * P], w_r[:, k, :],
                                   start=(k == 0), stop=(k == KD - 1))
            mm.then_inc(lg_full, 1)

            def gate_up(s, e, slot, c):
                if c == 0:
                    pe.wait_ge(s_e[slot], (e - slot) * 16 + 32)
                wait(pe, hm_done, s - 1)
                for half in range(2):
                    for k in range(KD):
                        mm = pe.matmul(gu_ps[:, c % 2, half, :], wgu[:, slot, k, half * EI:(half + 1) * EI],
                                       xT[:, k, c * CH:(c + 1) * CH], start=(k == 0), stop=(k == KD - 1))
                    mm.then_inc(gu_full, 1)

            def down(s, slot, c):
                pe.wait_ge(hm_done, s + 1)
                wait(pe, acc_done, TS * (s - 1))
                if c < 2:
                    pe.wait_ge(comb_done, 1)
                for t in range(TS):
                    mm = pe.matmul(dn_ps[:, c % 2, t, :], hm[:, c % 2, t * P:(t + 1) * P], wd[:, slot, :],
                                   start=True, stop=True)
                mm.then_inc(dn_full, 1)

            def pair(e, first):
                for j in range(2 * NCH):
                    s = NCH * e + j
                    gate_up(s, e + j // NCH, j // NCH, j % NCH)
                    if j > 0 or not first:
                        down(s - 1, (j - 1) // NCH % 2, (j - 1) % NCH)

            pair(0, True)
            with pe.Fori(1, EX // 2) as i:
                pair(2 * i, False)
            down(EX * NCH - 1, 1, NCH - 1)

        @block.scalar
        def _(act):
            for b in range(0, KD * NCH, 2):
                act.wait_ge(tr_full, b + 2)
                c = b // KD
                act.activation(xT[:, :, c * CH:(c + 1) * CH], gu_ps[:, b % 4 // 2, :, :],
                               ACT.Copy).then_inc(tr_free, 2)
            act.wait_ge(route, 2)
            act.activation(lg[:], lg[:], ACT.Exp).then_inc(exp_done, 1)

            def silu(s, c):
                act.wait_ge(gu_full, 2 * s + 1)
                wait(act, hm_done, s - 1)
                act.activation(sg[:, c % 2, :], gu_ps[:, c % 2, 0, :], ACT.Silu).then_inc(sg_done, 1)

            def pair(e):
                for j in range(2 * NCH):
                    silu(NCH * e + j, j % NCH)

            pair(0)
            with act.Fori(1, EX // 2) as i:
                pair(2 * i)

        @block.gpsimd
        def _(pool):
            pool.wait_ge(var_done, 1)
            pool.tensor_tensor(rstd[:], var[:], half[:], ALU.pow).then_inc(rstd_done, 1)

        @block.vector
        def _(ve):
            n = [0]

            def then(ins):
                n[0] += 1
                ins.then_inc(route, 1)
                ve.wait_ge(route, n[0])

            def rows(a):
                return a.unsqueeze(2).to_broadcast([P, NT, E])

            ve.wait_ge(lg_full, 1)
            ve.wait_ge(s_w, 32)
            lg_ps = dn_ps[:].rearrange("p a t d -> p (a t d)").rearrange("p (j e) -> p j e", e=E)
            then(ve.tensor_reduce(rs[:], lg_ps[:, 0:NT, :], AX.X, ALU.max))
            then(ve.tensor_tensor(lg[:], lg_ps[:, 0:NT, :], rows(rs[:]), ALU.subtract))
            ve.wait_ge(exp_done, 1)
            then(ve.tensor_reduce(rs[:], lg[:], AX.X, ALU.add))
            then(ve.reciprocal(rs[:], rs[:]))
            then(ve.tensor_tensor(lg[:], lg[:], rows(rs[:]), ALU.mult))
            ve.memset(corr[:, :, E:], NEVER)
            ve.memset(comb[:, :, E:], 1.0)
            then(ve.tensor_tensor(corr[:, :, 0:E], lg[:], bias[:].unsqueeze(1).to_broadcast([P, NT, E]), ALU.add))
            for j in range(NT):
                last = ve.max(top[:, j, :], corr[:, j, 0:E])
            then(last)
            then(ve.memset(top[:, :, TOPK:], NEVER))
            for j in range(NT):
                last = ve.match_replace(zap[:, j, :], top[:, j, :], corr[:, j, :], ZAPPED)
            then(last)
            then(ve.tensor_tensor(zap[:, :, 0:E], zap[:, :, 0:E], corr[:, :, 0:E], ALU.not_equal))
            then(ve.tensor_tensor(lg[:], lg[:], zap[:, :, 0:E], ALU.mult))
            then(ve.tensor_reduce(rs[:], lg[:], AX.X, ALU.add))
            then(ve.tensor_scalar(rs[:], rs[:], NORM_MIN, None, ALU.max))
            then(ve.reciprocal(rs[:], rs[:]))
            ve.tensor_tensor(comb[:, :, 0:E], lg[:], rows(rs[:]), ALU.mult).then_inc(comb_done, 1)
            ve.wait_ge(comb_done, 1)

            def product(s, c):
                ve.wait_ge(sg_done, s + 1)
                ve.wait_ge(gu_full, 2 * s + 2)
                wait(ve, dn_full, s - 1)
                ve.tensor_tensor(hm[:, c % 2, :], sg[:, c % 2, :], gu_ps[:, c % 2, 1, :], ALU.mult).then_inc(hm_done, 1)

            def accumulate(s, e, c):
                ve.wait_ge(dn_full, s + 1)
                for t in range(TS):
                    j = c * TS + t
                    w = comb[:, j, bass.ds(e, 1)]
                    ve.scalar_tensor_tensor(xkeep[:, j, :], dn_ps[:, c % 2, t, :], w, xkeep[:, j, :],
                                            ALU.mult, ALU.add).then_inc(acc_done, 1)

            def pair(e, first):
                for j in range(2 * NCH):
                    s = NCH * e + j
                    product(s, j % NCH)
                    if j > 0:
                        accumulate(s - 1, e + (j - 1) // NCH, (j - 1) % NCH)
                    elif not first:
                        accumulate(s - 1, e - 1, NCH - 1)

            pair(0, True)
            with ve.Fori(1, EX // 2) as i:
                pair(2 * i, False)
            accumulate(EX * NCH - 1, EX - 1, NCH - 1)

            ve.wait_ge(acc_done, EX * NT)
            for j in range(NT):
                ve.bn_stats(stats[:, j, :], xkeep[:, j, :]).then_inc(ln_step, 1)
            for j in range(NT):
                ve.wait_ge(ln_step, j + 1)
                ve.bn_aggr(mv[:, j, :], stats[:, j, :]).then_inc(ln_step, 1)
            ve.wait_ge(ln_step, 2 * NT)
            ve.memset(half[:], -0.5)
            ve.tensor_scalar(var[:], mv[:, :, 1], LN_EPS, None, ALU.add).then_inc(var_done, 1)
            ve.wait_ge(rstd_done, 1)
            for j in range(NT):
                ve.tensor_scalar(xkeep[:, j, :], xkeep[:, j, :], mv[:, j, 0:1], rstd[:, j:j + 1],
                                 ALU.subtract, ALU.mult).then_inc(y_done, 1)


def build(nc, A, out):
    with nc.sbuf_tensor("xkeep", [P, NT, D], F32) as xkeep, nc.sbuf_tensor("identity", [P, P], F32) as ident:
        mamba(nc, A, xkeep, ident)
        experts(nc, A, out, xkeep, ident)


def kernel(**inputs):
    import numpy as np
    import concourse.bacc as bacc
    from concourse.bass_utils import run_bass_kernel_spmd

    def T(a):
        return np.swapaxes(np.asarray(a), -1, -2)

    w = {k.replace("L0_attn_", "").replace("L0_ffn_", ""): np.asarray(v) for k, v in inputs.items()}
    x = w["x"].reshape(L, D)
    gu = np.concatenate([w["gate_up_proj"],
                         np.concatenate([w["shared_gate_w"].reshape(2, EI, D), w["shared_up_w"].reshape(2, EI, D)], 1)])
    down = np.concatenate([T(w["down_proj"]), T(w["shared_down_w"]).reshape(2, EI, D)])
    arrays = {
        "x": x, "xT": T(x), "W_inT": T(w["W_in"]), "W_dtT": T(w["W_dt"]), "W_outT": T(w["W_out"]),
        "W_BC3T": T(np.concatenate([w["W_B"], w["W_C"]] * 3)), "W_conv": w["W_conv"].reshape(DI, TAPS),
        "b_conv": w["b_conv"].reshape(KI, P).T, "b_dt": w["b_dt"].reshape(KI, P).T, "A_log": w["A_log"],
        "router_T": T(w["router_weight"]), "router_bias": w["e_score_bias"],
        "guT": T(gu), "dT": down,
        "ident": np.eye(P, dtype=np.float32), "sel3": np.tile(np.eye(BC, dtype=np.float32), (3, 1)),
    }
    arrays = {k: np.ascontiguousarray(v) for k, v in arrays.items()}
    nc = bacc.Bacc("TRN2", target_bir_lowering=False, num_devices=1)
    A = {k: nc.dram_tensor(k + "_d", v.shape, F32, kind="ExternalInput").ap() for k, v in arrays.items()}
    out = nc.dram_tensor("out_d", (L, D), F32, kind="ExternalOutput").ap()
    build(nc, A, out)
    r = run_bass_kernel_spmd(nc, [{k + "_d": v for k, v in arrays.items()}], core_ids=[0])
    return np.asarray(r.results[0]["out_d"]).reshape(1, L, D)
```

```python
from contextlib import ExitStack

import concourse.bass as bass
from concourse import mybir

F32 = mybir.dt.float32
BF16 = mybir.dt.bfloat16
I32 = mybir.dt.int32
U32 = mybir.dt.uint32
ALU = mybir.AluOpType
ACT = mybir.ActivationFunctionType
AX = mybir.AxisListType

P = 128
D = 256
DI = 512
NST = 16
TAPS = 4
L = 4096
CH = 512
NCH = L // CH
KD = D // P
KI = DI // P
TS = CH // P
NT = L // P
E = 32
EI = 128
TOPK = 6
LN_EPS = 1e-5
NEVER, ZAPPED = -3.0e38, -3.2e38
NORM_MIN = 1e-12
CAP = L + P
ROW = D + 2 * E
NTILE = (L * TOPK) // P + E
BC = 2 * NST

FROM = 1

SW = 2 * NST
HR = 4
MH = KI // 2
HD = DI // 2

PE_STEPS = {
    0: [("RX", 0), ("RX", 1)], 1: [("IN", 0)], 2: [("IN", 1)], 3: [("IN", 2)], 4: [("IN", 3)],
    5: [("LG", 1), ("Z", 0)], 6: [("Z", 1)], 7: [("Z", 2)], 8: [("Z", 3)],
    9: [("RK", 0)], 10: [("GT", 0), ("GT", 1)], 11: [("GT", 2), ("GT", 3)],
    12: [("BC", 0)], 14: [("DT", 0)], 16: [("DT", 1)], 18: [("DT", 2)], 20: [("DT", 3)],
    22: [("OUT", 1)], 24: [("OUT", 0)],
}
LONG = {"BC", "DT"}
AHEAD = {"IN", "BC", "DT"}
BEHIND = {"GT", "OUT"}
LATE = {"RX", "LG", "RK", "PROB", "CHOOSE", "PLACE", "SCATTER"}
ACT_STEPS = {
    2: [("RX", 0), ("RX", 1)], 3: [("IN", 0)], 4: [("IN", 1)], 5: [("IN", 2)], 6: [("IN", 3)],
    7: [("Z", 0)], 8: [("PROB", 0), ("Z", 1)], 9: [("Z", 2)], 10: [("Z", 3), ("TANH", 0)],
    11: [("TANH", 1), ("TANH", 2)], 12: [("TANH", 3), ("GT", 0)], 13: [("GT", 1), ("GT", 2)], 14: [("GT", 3)],
    15: [("BC", 0)], 17: [("DT", 0)], 18: [("ABS", 0)], 19: [("EXP", 0)], 20: [("DT", 1)], 21: [("ABS", 1)],
    22: [("DT", 2), ("EXP", 1)], 23: [("ABS", 2)], 24: [("DT", 3), ("EXP", 2)], 25: [("ABS", 3)],
    26: [("EXP", 3), ("LN", 0)], 27: [("LN", 1), ("LN", 2)], 28: [("LN", 3)],
}
VE_STEPS = {
    1: [("GATE", 1)],
    7: [("LG", 1), ("CONV", 1)], 8: [("Z", 0), ("CONV", 2), ("CONV", 3)], 9: [("CHOOSE", 0), ("Z", 1)],
    10: [("Z", 2)], 11: [("PLACE", 0), ("Z", 3)], 12: [("SILU", 0), ("SILU", 1)], 13: [("SILU", 2), ("SILU", 3)],
    16: [("BC", 0)], 17: [("GATE", 0)], 25: [("OUT", 1)], 27: [("OUT", 0), ("STATS", 0)],
    28: [("SOFT", 0)], 29: [("SOFT", 1), ("SOFT", 2)], 30: [("SOFT", 3), ("NORM", 0)],
}
AFTER = BEHIND | LATE | {"STATS", "NORM", "RSTD"}
SCATTERS = {13: 3, 14: 1, 15: 1, 16: 1, 17: 1, 18: 4, 19: 1, 20: 1, 21: 1, 22: 1, 23: 1, 24: 1, 25: 1, 27: 2,
            28: 1, 29: 3}
assert sum(SCATTERS.values()) == TS * TOPK
POOL_STEPS = {s: [("SCATTER", sum(n for v, n in SCATTERS.items() if v < s) + k) for k in range(SCATTERS.get(s, 0))]
              for s in range(SW)}
POOL_STEPS[SW - 3] += [("RSTD", 0)]
AGAIN = 100
MOVED = ("OUT", "STATS", "NORM", "RSTD")


def last_steps(steps, more):
    kept = {s: [u for u in of if u[0] not in MOVED] for s, of in steps.items()}
    return {s: kept.get(s, []) + more.get(s, []) for s in range(SW)}


LAST = {id(steps): last_steps(steps, more) for steps, more in (
    (PE_STEPS, {14: [("OUT", 0)], 15: [("OUT", 1)], 20: [("RX", AGAIN), ("RX", AGAIN + 1)], 22: [("LG", AGAIN + 1)],
                26: [("RK", AGAIN)]}),
    (ACT_STEPS, {21: [("RX", AGAIN), ("RX", AGAIN + 1)], 24: [("PROB", AGAIN)]}),
    (VE_STEPS, {16: [("OUT", 0)], 17: [("OUT", 1), ("STATS", 0)], 19: [("NORM", 0)], 23: [("LG", AGAIN + 1)],
                25: [("CHOOSE", AGAIN)], 27: [("PLACE", AGAIN)]}),
    (POOL_STEPS, {18: [("RSTD", 0)]}),
)}
AHEAD_TOO = AHEAD | {"TANH", "ABS", "EXP", "LN", "CONV", "SILU", "SOFT"}
BEHIND_TOO = BEHIND | {"STATS", "NORM", "RSTD"}
PROLOGUE = [("IN", m) for m in range(KI)] + [("BC", 0)] + [("DT", m) for m in range(KI)]
EPILOGUE = ([("GT", m) for m in range(KI)] + [("OUT", 0), ("OUT", 1)] + [("RX", 0), ("RX", 1), ("LG", 1), ("RK", 0)]
            + [("TOTAL", 1)])


def bank(use):
    return (use[1] + (use[0] == "DT")) % 2


def tasks(steps, s, ahead, behind, late):
    if not ahead:
        steps = LAST[id(steps)]
    return [u for u in steps.get(s, []) if (ahead or u[0] not in AHEAD_TOO) and (behind or u[0] not in BEHIND_TOO)
            and (late or u[0] not in LATE)]


def chunk_of(u, c, par):
    if u[0] in AHEAD_TOO:
        return c + 1, 1 - par
    if u[0] in BEHIND_TOO or (u[0] in LATE and u[1] >= AGAIN):
        return c - 1, 1 - par
    if u[0] in LATE:
        return c - 2, par
    return c, par


def body_uses(b, when):
    return [u for s in range(SW) for u in tasks(PE_STEPS, s, *when) if bank(u) == b]


def px_base(b, c):
    base = len([u for u in PROLOGUE if bank(u) == b])
    if isinstance(c, int) and c < 2:
        return base + (len(body_uses(b, (True, False, False))) if c else 0)
    return (base + len(body_uses(b, (True, False, False))) + len(body_uses(b, (True, True, False)))
            + (c - 2) * len(body_uses(b, (True, True, True))))


def use_no(u, c, when):
    b = bank(u)
    if isinstance(c, str) and c == "prologue":
        return [v for v in PROLOGUE if bank(v) == b].index(u)
    if isinstance(c, str) and c == "epilogue":
        before = px_base(b, NCH - 1) + len(body_uses(b, (False, True, True)))
        return before + [v for v in EPILOGUE if bank(v) == b].index(u)
    return px_base(b, c) + body_uses(b, when).index(u)


def transposes_of(u, c, when):
    if u[0] == "OUT":
        return [use_no(("GT", KI - 2 + v), c, when) for v in (0, 1)]
    if u[0] == "LG":
        return [use_no(("RX", u[1] - 1 + v), c, when) for v in (0, 1)]
    return None


def wait(eng, sem, value):
    if isinstance(value, int) and value <= 0:
        return
    eng.wait_ge(sem, value)


def chunks(eng, body):
    body(0, 0, (True, False, False))
    body(1, 1, (True, True, False))
    with eng.Fori(1, (NCH - 2) // 2) as i:
        body(2 * i, 0, (True, True, True))
        body(2 * i + 1, 1, (True, True, True))
    body(NCH - 2, 0, (True, True, True))
    body(NCH - 1, 1, (False, True, True))


class AfterScan:

    def __init__(self, nc, ctx, A):
        def sb(name, shape, dt=F32):
            return ctx.enter_context(nc.sbuf_tensor(name, shape, dt))

        def sem(name):
            return ctx.enter_context(nc.semaphore(name))

        self.ident = sb("identity", [P, P])
        self.g = sb("g", [P, TS, DI])
        self.gT = sb("gT", [P, KI, CH])
        self.w_out = sb("w_out", [P, KI, D])
        self.xr = sb("xr", [P, TS, D])
        self.stats = sb("stats", [P, TS, 6])
        self.mv = sb("mv", [P, TS, 2])
        self.var = sb("var", [P, TS])
        self.half_c = sb("half_c", [P, TS])
        self.rstd = sb("rstd", [P, TS])
        self.x1 = sb("x1", [P, 2, TS, ROW])
        self.pads = sb("pads", [P, ROW])
        self.place0 = sb("place0", [P, TS])
        self.x1T = sb("x1T", [P, KD, CH])
        self.w_r = sb("w_r", [P, KD, E])
        self.bias = sb("bias", [P, E])
        self.region = sb("region", [P, E])
        self.tri_f = sb("tri_f", [P, P])
        self.tri = sb("tri", [P, P], BF16)
        self.ones = sb("ones", [P, P], BF16)
        self.prob = sb("prob", [P, TS, E])
        self.chosen = sb("chosen", [P, TS, E])
        self.mask = sb("mask", [P, TS, E], BF16)
        self.one_row = sb("one_row", [P, E])
        self.masks = sb("masks", [P, E], BF16)
        self.msum = sb("msum", [P, E])
        self.corr = sb("corr", [P, TS, E + 2])
        self.zap = sb("zap", [P, TS, E + 2])
        self.top = sb("top", [P, TS, 8])
        self.rs = sb("rs", [P, TS])
        self.rows_at = sb("rows_at", [P, 2, TS, TOPK], U32)
        self.px = ctx.enter_context(nc.psum_tensor("px", [P, 2, CH], F32))
        self.x1_d = nc.dram_tensor("x1_rows", (L, D), F32, kind="Internal").ap()
        self.rows_d = nc.dram_tensor("expert_rows", (E * CAP, ROW), F32, kind="Internal").ap()

        self.s_xr = sem("xr_landed")
        self.s_route = sem("routing_constants_landed")
        self.px_full = [sem(f"px_full{i}") for i in range(2)]
        self.px_free = [sem(f"px_free{i}") for i in range(2)]
        self.g_done = sem("g_done")
        self.ln_step = sem("ln_step")
        self.seen = sem("wait_seen")
        self.var_done = sem("var_done")
        self.rstd_done = sem("rstd_done")
        self.x1_done = sem("x1_done")
        self.x1_stored = sem("x1_stored")
        self.logits_read = sem("logits_read")
        self.exp_done = sem("route_exp_done")
        self.route = sem("route_step")
        self.mask_done = sem("mask_done")
        self.rows_ready = sem("rows_ready")
        self.scattered = [sem(f"scattered{i}") for i in range(2)]


    def load_constants(self, sp, A):
        for dst, src in (
            (self.w_r[:], A["router_T"].rearrange("(k p) e -> p k e", p=P)),
            (self.bias[:], A["router_bias"].partition_broadcast(P)),
            (self.region[:], A["region1"].partition_broadcast(P)),
            (self.tri_f[:], A["before"]),
            (self.place0[:], A["place0"]),
            (self.pads[:], A["pads"]),
        ):
            sp.dma_start(dst, src).then_inc(self.s_route, 16)

    def store_rows(self, sp, o, par):
        sp.wait_ge(self.x1_done, TS * (o + 1))
        sp.dma_start(self.x1_d.rearrange("(j p) d -> p j d", p=P)[:, bass.ds(o * TS, TS), :],
                     self.x1[:, par, :, 0:D]).then_inc(self.x1_stored, 16)


    def tensor_use(self, pe, u, q, qpar, i, before=None):
        kind, m = u
        m = m % AGAIN
        b = bank(u)
        px = self.px
        if kind == "GT" and m == 0:
            pe.wait_ge(self.g_done, 2 * TS * (q + 1))
        if kind == "RX" and m == 0:
            pe.wait_ge(self.x1_done, TS * (q + 1))
        if kind in ("OUT", "LG"):
            for v in (0, 1):
                pe.wait_ge(self.px_free[v], before[v] + 1)
        if kind == "RK":
            pe.wait_ge(self.mask_done, q + 1)
        wait(pe, self.px_free[b], i)
        if kind in ("GT", "RX"):
            for t in range(TS):
                src = self.g[:, t, m * P:(m + 1) * P] if kind == "GT" else self.x1[:, qpar, t, m * P:(m + 1) * P]
                mm = pe.transpose(px[:, b, t * P:(t + 1) * P], src, self.ident[:])
        elif kind == "OUT":
            for t in range(2):
                ts = 2 * m + t
                for k in range(KI):
                    mm = pe.matmul(px[:, b, t * D:(t + 1) * D], self.gT[:, k, ts * P:(ts + 1) * P], self.w_out[:, k, :],
                                   start=(k == 0 and t == 0), stop=(k == KI - 1), skip_group_check=True)
        elif kind == "LG":
            pe.wait_ge(self.s_route, 16 * 6)
            for t in range(TS):
                for k in range(KD):
                    mm = pe.matmul(px[:, b, t * E:(t + 1) * E], self.x1T[:, k, t * P:(t + 1) * P], self.w_r[:, k, :],
                                   start=(k == 0 and t == 0), stop=(k == KD - 1), skip_group_check=True)
        elif kind == "RK":
            for t in range(TS):
                terms = [(self.ones, self.masks[:])]
                terms += [(self.ones, self.mask[:, v, :]) for v in range(t)]
                terms += [(self.tri, self.mask[:, t, :])]
                for n, (lhsT, rhs) in enumerate(terms):
                    mm = pe.matmul(px[:, b, t * E:(t + 1) * E], lhsT[:], rhs, start=(n == 0 and t == 0),
                                   stop=(n == len(terms) - 1), skip_group_check=True)
        else:
            pe.wait_ge(self.rows_ready, q + 1)
            mm = pe.matmul(px[:, b, 0:E], self.ones[:], self.masks[:], start=True, stop=True)
        mm.then_inc(self.px_full[b], 1)


    def scalar_task(self, act, u, q, i):
        kind, m = u
        m = m % AGAIN
        b = bank(u)
        if kind == "PROB":
            act.wait_ge(self.logits_read, q + 1)
            act.activation(self.prob[:], self.prob[:], ACT.Exp).then_inc(self.exp_done, 1)
            return
        act.wait_ge(self.px_full[b], i + 1)
        dst = self.gT[:, m, :] if kind == "GT" else self.x1T[:, m, :]
        act.activation(dst, self.px[:, b, :], ACT.Copy).then_inc(self.px_free[b], 1)


    def pad_regions(self, pool):
        pool.sem_inc(self.x1_stored, FROM)
        pool.wait_ge(self.s_route, 16 * 6)
        starts = self.rows_d.rearrange("(e c) d -> c e d", c=CAP)[0:P]
        for par in range(2):
            pool.dma_start(starts[:, par * E // 2:(par + 1) * E // 2],
                           self.pads[:].unsqueeze(1).to_broadcast([P, E // 2, ROW])).then_inc(self.scattered[par], 16)

    def pool_task(self, pool, u, q, qpar):
        kind, m = u
        m = m % AGAIN
        if kind == "RSTD":
            pool.wait_ge(self.var_done, q + 1)
            pool.tensor_tensor(self.rstd[:], self.var[:], self.half_c[:], ALU.pow).then_inc(self.rstd_done, 1)
        else:
            if m == 0:
                pool.wait_ge(self.rows_ready, q + 1)
                pool.sem_inc(self.seen, 1)
            t, k = m // TOPK, m % TOPK
            pool.indirect_dma_start(self.rows_d, bass.IndirectOffsetOnAxis(self.rows_at[:, qpar, t, k:k + 1], 0),
                                    self.x1[:, qpar, t, :], None).then_inc(self.scattered[qpar], 16)


    ROUTE_STEPS = 21

    def vector_task(self, ve, u, q, qpar, i):
        kind, m = u
        m = m % AGAIN
        b = bank(u)
        x1, xr, mv, stats = self.x1, self.xr, self.mv, self.stats
        prob, chosen = self.prob[:], self.chosen[:]
        slots, zap, top, rs = self.corr[:, :, 0:E], self.zap[:, :, 0:E], self.top, self.rs
        px3 = self.px[:, b, 0:TS * E].rearrange("p (t e) -> p t e", e=E)

        def then(ins, alone=False):
            self.n += 1
            ins.then_inc(self.route, 1)
            ve.wait_ge(self.route, self.ROUTE_STEPS * q + self.n)
            if alone:
                ve.sem_inc(self.seen, 1)

        def rows(a):
            return a.unsqueeze(2).to_broadcast([P, TS, E])

        def cols(a):
            return a.unsqueeze(1).to_broadcast([P, TS, E])

        if kind == "OUT":
            ve.wait_ge(self.px_full[b], i + 1)
            ve.wait_ge(self.s_xr, 16 * (q + 1))
            r = xr[:, 2 * m:2 * m + 2, :]
            ve.tensor_tensor(r, self.px[:, b, :].rearrange("p (t d) -> p t d", t=2), r,
                             ALU.add).then_inc(self.px_free[b], 1)
        elif kind == "STATS":
            for v in (0, 1):
                ve.wait_ge(self.px_free[bank(("OUT", v))], i[v] + 1)
            for t in range(TS):
                ve.bn_stats(stats[:, t, :], xr[:, t, :]).then_inc(self.ln_step, 1)
            ve.wait_ge(self.ln_step, 2 * TS * q + TS)
            ve.sem_inc(self.seen, 1)
            for t in range(TS):
                ve.bn_aggr(mv[:, t, :], stats[:, t, :]).then_inc(self.ln_step, 1)
            ve.wait_ge(self.ln_step, 2 * TS * (q + 1))
            ve.tensor_scalar(self.var[:], mv[:, :, 1], LN_EPS, None, ALU.add).then_inc(self.var_done, 1)
        elif kind == "NORM":
            ve.wait_ge(self.rstd_done, q + 1)
            if not (isinstance(q, int) and q < 2):
                ve.wait_ge(self.x1_stored, 16 * (q - 1) + FROM)
                ve.wait_ge(self.scattered[qpar], (q - qpar) * (8 * TS * TOPK) + 16)
            for t in range(TS):
                ve.tensor_scalar(x1[:, qpar, t, 0:D], xr[:, t, :], mv[:, t, 0:1], self.rstd[:, t:t + 1],
                                 ALU.subtract, ALU.mult).then_inc(self.x1_done, 1)
        elif kind == "LG":
            self.n = 0
            ve.wait_ge(self.px_full[b], i + 1)
            then(ve.tensor_reduce(rs[:], px3, AX.X, ALU.max))
            ins = ve.tensor_tensor(prob, px3, rows(rs[:]), ALU.subtract)
            ins.then_inc(self.px_free[b], 1)
            ve.wait_ge(self.px_free[b], i + 1)
            ve.sem_inc(self.logits_read, 1)
        elif kind == "CHOOSE":
            ve.wait_ge(self.exp_done, q + 1)
            ve.sem_inc(self.seen, 1)
            then(ve.tensor_reduce(rs[:], prob, AX.X, ALU.add), alone=True)
            then(ve.reciprocal(rs[:], rs[:]))
            then(ve.tensor_tensor(prob, prob, rows(rs[:]), ALU.mult))
            then(ve.tensor_tensor(slots, prob, cols(self.bias[:]), ALU.add), alone=True)
            for t in range(TS):
                last = ve.max(top[:, t, :], self.corr[:, t, 0:E])
            then(last, alone=True)
            then(ve.memset(top[:, :, TOPK:], NEVER), alone=True)
            for t in range(TS):
                last = ve.match_replace(self.zap[:, t, :], top[:, t, :], self.corr[:, t, :], ZAPPED)
            then(last)
            then(ve.tensor_tensor(chosen, zap, slots, ALU.not_equal))
            ve.tensor_copy(self.mask[:], chosen).then_inc(self.mask_done, 1)
            then(ve.tensor_tensor(prob, prob, chosen, ALU.mult), alone=True)
            then(ve.tensor_reduce(rs[:], prob, AX.X, ALU.add))
            then(ve.tensor_scalar(rs[:], rs[:], NORM_MIN, None, ALU.max), alone=True)
            then(ve.reciprocal(rs[:], rs[:]))
            ve.tensor_tensor(x1[:, qpar, :, D + E:], prob, rows(rs[:]), ALU.mult)
            for t in range(TS):
                last = ve.tensor_tensor_scan(x1[:, qpar, t, D:D + E], self.one_row[:], chosen[:, t, :],
                                             self.place0[:, t:t + 1], ALU.mult, ALU.add)
            then(last)
            then(ve.tensor_scalar(self.place0[:], self.place0[:], float(TOPK * CH), None, ALU.add))
        elif kind == "PLACE":
            ve.wait_ge(self.px_full[b], i + 1)
            ve.tensor_tensor(zap, px3, cols(self.region[:]), ALU.add).then_inc(self.px_free[b], 1)
            ve.wait_ge(self.px_free[b], i + 1)
            ve.sem_inc(self.seen, 1)
            then(ve.tensor_tensor(slots, zap, chosen, ALU.mult), alone=True)
            for t in range(TS):
                last = ve.max(top[:, t, :], self.corr[:, t, 0:E])
            then(last)
            if not (isinstance(q, int) and q < 2):
                ve.wait_ge(self.scattered[qpar], (q - qpar) * (8 * TS * TOPK) + 16)
            then(ve.tensor_scalar(self.rows_at[:, qpar], top[:, :, 0:TOPK], -1.0, None, ALU.add), alone=True)
            then(ve.tensor_reduce(self.msum[:], chosen.rearrange("p t e -> p e t"), AX.X, ALU.add))
            then(ve.tensor_tensor(self.msum[:], self.msum[:], self.masks[:], ALU.add))
            then(ve.tensor_copy(self.masks[:], self.msum[:]), alone=True)
            ve.sem_inc(self.rows_ready, 1)
            assert self.n == self.ROUTE_STEPS, self.n

    def vector_constants(self, ve):
        ve.memset(self.half_c[:], -0.5)
        ve.memset(self.ones[:], 1.0)
        ve.memset(self.masks[:], 0.0)
        ve.memset(self.one_row[:], 1.0)
        ve.memset(self.corr[:, :, E:], NEVER)
        ve.wait_ge(self.s_route, 16 * 6)
        ve.tensor_copy(self.tri[:], self.tri_f[:])


def mamba(nc, A, after):
    with ExitStack() as ctx:
        def sb(name, shape, dt=F32):
            return ctx.enter_context(nc.sbuf_tensor(name, shape, dt))

        def sem(name):
            return ctx.enter_context(nc.semaphore(name))

        g, xr, ident, w_out = after.g, after.xr, after.ident, after.w_out
        px, px_full, px_free, g_done = after.px, after.px_full, after.px_free, after.g_done
        w_in = sb("w_in", [P, KD, 2 * DI])
        w_dt = sb("w_dt", [P, KI, DI])
        w_bc = sb("w_bc", [P, KI, 3 * BC])
        w_conv = sb("w_conv", [P, KI, TAPS])
        b_conv = sb("b_conv", [P, KI])
        b_dt = sb("b_dt", [P, KI])
        a_neg = sb("a_neg", [P, KI, NST])
        sel_f = sb("sel_f", [3 * BC, BC])
        sel = sb("sel", [3 * BC, BC], BF16)
        xT = sb("xT", [P, 2, KD, CH])
        xin = sb("xin", [P, KI, TAPS - 1 + CH])
        u_sb = sb("u", [P, KI, CH])
        scr = sb("scr", [P, KI, CH])
        vb = sb("vb", [P, KI, CH])
        dt = sb("dt", [P, 2, KI, CH])
        dtu = sb("dtu", [P, KI, CH])
        dbu = sb("dbu", [P, 2, MH, CH])
        h = sb("h", [P, HR, MH, CH])
        hc = sb("hc", [P, 2, MH, CH])
        zg = sb("zg", [P, TS, DI])
        thz = scr[:, KI - 1, :]
        bb = sb("bb", [P, NST, CH])
        brow = scr[0:NST, 1, :]
        bc3 = sb("bc3", [3 * BC, 2, CH], BF16)
        bcr = scr[0:3 * BC, 0, :]
        b_dram = nc.dram_tensor("b_rows", (2, NST, CH), F32, kind="Internal").ap()
        carry = sb("carry", [P, NST, KI])
        y_ps = ctx.enter_context(nc.psum_tensor("y_ps", [P, TS, HD], F32))
        da_ps = ctx.enter_context(nc.psum_tensor("da_ps", [P, 2, CH], F32))
        cb_ps = ctx.enter_context(nc.psum_tensor("cb_ps", [P, 2, CH], F32))

        s_w = sem("weights_landed")
        s_xT = [sem(f"xT_landed{i}") for i in range(2)]
        brow_done = sem("brow_done")
        brow_stored = sem("brow_stored")
        bb_landed = [sem(f"bb_landed{i}") for i in range(NST)]
        prep = sem("prep_act")
        prepv = sem("prep_vector")
        tap0_done = sem("tap0_done")
        conv_step = sem("conv_step")
        head_done = sem("head_done")
        tanh_u = sem("tanh_u_done")
        u_done = sem("u_done")
        bc_hi = sem("bc_hi_done")
        bc_step = sem("bc_step")
        soft_abs = sem("soft_abs_done")
        soft_exp = sem("soft_exp_done")
        soft_log = sem("soft_log_done")
        dt_done = sem("dt_done")
        dtu_done = sem("dtu_done")
        dbu_done = sem("dbu_done")
        da_full = sem("da_full")
        scan_done = sem("scan_done")
        carry_done = sem("carry_done")
        cb_full = sem("cb_full")
        hc_done = sem("hc_done")
        ytr_done = sem("ytr_done")
        tanh_z = sem("tanh_z_done")

        block = ctx.enter_context(nc.Block())
        NW = 10

        @block.sync
        def _(sp):
            for dst, src in (
                (w_in[:], A["W_inT"].rearrange("(k p) n -> p k n", p=P)),
                (w_conv[:], A["W_conv"].rearrange("(m p) t -> p m t", p=P)),
                (b_conv[:], A["b_conv"]),
                (b_dt[:], A["b_dt"]),
                (w_bc[:], A["W_BC3T"].rearrange("(k p) n -> p k n", p=P)),
                (a_neg[:], A["A_log"].rearrange("(m p) s -> p m s", p=P)),
                (w_dt[:], A["W_dtT"].rearrange("(k p) n -> p k n", p=P)),
                (sel_f[:], A["sel3"]),
                (ident[:], A["ident"]),
                (w_out[:], A["W_outT"].rearrange("(k p) n -> p k n", p=P)),
            ):
                sp.dma_start(dst, src).then_inc(s_w, 16)
            after.load_constants(sp, A)
            xT_d = A["xT"].rearrange("(k p) t -> p k t", p=P)
            x_d = A["x"].rearrange("(j p) d -> p j d", p=P)
            sp.dma_start(xT[:, 0], xT_d[:, :, 0:CH]).then_inc(s_xT[0], 16)

            def load_rows(o):
                wait(sp, after.x1_done, TS * o)
                sp.dma_start(xr[:], x_d[:, bass.ds(o * TS, TS), :]).then_inc(after.s_xr, 16)

            def spread_rows(q, qpar):
                sp.wait_ge(brow_done, q + 1)
                sp.dma_start(b_dram[qpar], brow[:]).then_inc(brow_stored, 16)
                sp.wait_ge(brow_stored, 16 * (q + 1))
                for n in range(NST):
                    wait(sp, dbu_done, SW * q - NST + n + 1)
                    sp.dma_start(bb[:, n, :], b_dram[qpar, n].partition_broadcast(P)).then_inc(bb_landed[n], 16)

            def load_xT(q, qpar):
                wait(sp, tanh_z, TS * (q - 1))
                sp.dma_start(xT[:, qpar], xT_d[:, :, bass.ds(q * CH, CH)]).then_inc(s_xT[qpar], 16)

            def body(c, par):
                if not (isinstance(c, int) and c < 2):
                    after.store_rows(sp, c - 2, par)
                if not (isinstance(c, int) and c == 0):
                    load_rows(c - 1)
                if not (isinstance(c, int) and c + 2 >= NCH):
                    load_xT(c + 2, par)
                spread_rows(c + 1, 1 - par)

            load_xT(1, 1)
            spread_rows(0, 0)
            body(0, 0)
            body(1, 1)
            with sp.Fori(1, (NCH - 2) // 2) as i:
                body(2 * i, 0)
                body(2 * i + 1, 1)
            body(NCH - 2, 0)
            after.store_rows(sp, NCH - 3, 1)
            load_rows(NCH - 2)
            after.store_rows(sp, NCH - 2, 0)
            load_rows(NCH - 1)

        @block.tensor
        def _(pe):
            def part(u, k0, k1, q, qpar, i):
                kind, m = u
                b = bank(u)
                out = px[:, b, :]
                last = k1 == (KD if kind in ("IN", "Z") else KI)
                if k0 == 0:
                    if kind == "IN" and m == 0:
                        pe.wait_ge(s_xT[qpar], (q - qpar) * 8 + 16)
                    if kind == "BC":
                        pe.wait_ge(u_done, KI * (q + 1))
                    wait(pe, px_free[b], i)
                for k in range(k0, k1):
                    if kind == "IN":
                        lhsT, rhs = w_in[:, k, m * P:(m + 1) * P], xT[:, qpar, k, :]
                    elif kind == "Z":
                        lhsT, rhs = xT[:, qpar, k, m * P:(m + 1) * P], w_in[:, k, DI:2 * DI]
                    elif kind == "BC":
                        lhsT, rhs, out = w_bc[:, k, :], u_sb[:, k, :], px[0:3 * BC, b, :]
                    else:
                        lhsT, rhs = w_dt[:, k, m * P:(m + 1) * P], u_sb[:, k, :]
                    mm = pe.matmul(out, lhsT, rhs, start=(k == 0), stop=(k == k1 - 1 and last))
                if last:
                    mm.then_inc(px_full[b], 1)

            def spread_c(c, s, par):
                n = s % NST
                if s == 0:
                    pe.wait_ge(bc_step, 3 * (c + 1))
                wait(pe, hc_done, SW * c + s - 1)
                pe.matmul(cb_ps[:, s % 2, :], sel[:, NST + n:NST + n + 1].to_broadcast([3 * BC, P]), bc3[:, par, :],
                          start=True, stop=True).then_inc(cb_full, 1)

            def sum_states(c, s):
                pe.wait_ge(hc_done, SW * c + s + 1)
                if s % NST == 0:
                    wait(pe, g_done, TS * (2 * c + s // NST))
                for t in range(TS):
                    for m in range(MH):
                        mm = pe.matmul(y_ps[:, t, m * P:(m + 1) * P], hc[:, s % 2, m, t * P:(t + 1) * P],
                                       ident[:], is_transpose=True, start=(s % NST == 0 and m == 0 and t % 2 == 0),
                                       stop=(s % NST == NST - 1 and m == MH - 1 and t % 2 == 1), skip_group_check=True)
                mm.then_inc(ytr_done, 1)

            pe.wait_ge(s_w, 16 * NW)
            pe.wait_ge(prepv, 3)
            for u in PROLOGUE:
                part(u, 0, KI if u[0] in LONG else KD, 0, 0, use_no(u, "prologue", None))
            spread_c(0, 0, 0)

            def body(c, par, when):
                ahead, behind, late = when
                for s in range(SW):
                    if s > 0:
                        sum_states(c, s - 1)
                    elif behind:
                        sum_states(c - 1, SW - 1)
                    if s + 1 < SW:
                        spread_c(c, s + 1, par)
                    elif ahead:
                        spread_c(c + 1, 0, 1 - par)
                    for first, at in ((False, s - 1), (True, s)):
                        for u in tasks(PE_STEPS, at, *when):
                            if not first and u[0] not in LONG:
                                continue
                            q, qpar = chunk_of(u, c, par)
                            i = use_no(u, c, when)
                            if u[0] in AFTER:
                                after.tensor_use(pe, u, q, qpar, i, transposes_of(u, c, when))
                            elif u[0] not in LONG:
                                part(u, 0, KD, q, qpar, i)
                            else:
                                part(u, 0 if first else KI // 2, KI // 2 if first else KI, q, qpar, i)

            chunks(pe, body)
            sum_states(NCH - 1, SW - 1)

        @block.scalar
        def _(act):
            def task(u, q, qpar, i, before=None):
                kind, m = u
                b = bank(u)
                if kind in ("IN", "Z", "BC", "DT"):
                    act.wait_ge(px_full[b], i + 1)
                if kind == "IN":
                    if m == 0:
                        act.wait_ge(head_done, q + 1)
                    act.activation(xin[:, m, TAPS - 1:], px[:, b, :], ACT.Copy).then_inc(px_free[b], 1)
                    wait(act, dtu_done, 2 * q)
                    act.sem_inc(after.seen, 1)
                    act.wait_ge(px_free[b], i + 1)
                    act.activation(u_sb[:, m, :], xin[:, m, 0:CH], ACT.Identity, scale=w_conv[:, m, 0:1],
                                   bias=b_conv[:, m:m + 1]).then_inc(tap0_done, 1)
                elif kind == "TANH":
                    act.wait_ge(conv_step, KI * (TAPS - 1) * q + KI * (TAPS - 2) + m + 1)
                    if before is not None:
                        act.wait_ge(px_free[bank(("Z", TS - 1))], before + 1)
                    act.activation(scr[:, m, :], u_sb[:, m, :], ACT.Tanh).then_inc(tanh_u, 1)
                elif kind == "BC":
                    wait(act, brow_stored, 16 * q)
                    act.activation(brow[:], px[0:NST, b, :], ACT.Copy).then_inc(brow_done, 1)
                    act.activation(bc3[:, qpar, :], px[0:3 * BC, b, :], ACT.Copy).then_inc(bc_hi, 1)
                elif kind == "DT":
                    wait(act, dt_done, KI * q)
                    act.activation(vb[:, m, :], px[:, b, :], ACT.Identity, bias=b_dt[:, m:m + 1]).then_inc(px_free[b], 1)
                elif kind == "ABS":
                    act.wait_ge(px_free[bank(("DT", m))], i + 1)
                    act.wait_ge(bc_step, 3 * (q + 1))
                    act.wait_ge(brow_stored, 16 * (q + 1))
                    act.activation(scr[:, m, :], vb[:, m, :], ACT.Abs).then_inc(soft_abs, 1)
                elif kind == "EXP":
                    act.wait_ge(soft_abs, KI * q + m + 1)
                    act.activation(scr[:, m, :], scr[:, m, :], ACT.Exp, scale=-1.0).then_inc(soft_exp, 1)
                elif kind == "LN":
                    act.wait_ge(soft_exp, KI * q + m + 1)
                    act.activation(scr[:, m, :], scr[:, m, :], ACT.Ln, bias=1.0).then_inc(soft_log, 1)
                elif kind == "Z":
                    if m > 0:
                        act.wait_ge(px_free[1 - b], before + 1)
                    act.activation(thz[:], px[:, b, :], ACT.Tanh).then_inc(tanh_z, 1)

            def decay(c, par, s, m):
                n, mt = s % NST, s // NST * MH + m
                if n == 0 and m == 0:
                    act.wait_ge(dt_done, KI * c + mt + MH)
                wait(act, scan_done, (SW * c + s) * MH + m - 1)
                act.activation(da_ps[:, m, :], dt[:, par, mt, :], ACT.Exp,
                               scale=a_neg[:, mt, n:n + 1]).then_inc(da_full, 1)

            def keep_state(c, s):
                n, m0 = s % NST, s // NST * MH
                act.wait_ge(scan_done, (SW * c + s + 1) * MH)
                act.activation(carry[:, n, m0:m0 + MH], h[:, s % HR, :, CH - 1], ACT.Copy).then_inc(carry_done, 1)

            act.wait_ge(s_w, 16 * NW)
            act.activation(a_neg[:], a_neg[:], ACT.Exp).then_inc(prep, 1)
            act.wait_ge(prepv, 4)
            order = [("IN", m) for m in range(KI)] + [("TANH", m) for m in range(KI)] + [("BC", 0)]
            order += [(kind, m) for m in range(KI) for kind in ("DT", "ABS", "EXP", "LN")]
            for kind, m in order:
                of = ("DT", m) if kind == "ABS" else (kind, m)
                task((kind, m), 0, 0, use_no(of, "prologue", None) if of in PROLOGUE else None)

            def body(c, par, when):
                ahead, behind, late = when
                for s in range(SW):
                    decay(c, par, s, 0)
                    if s > 0:
                        keep_state(c, s - 1)
                    elif behind:
                        keep_state(c - 1, SW - 1)
                    decay(c, par, s, 1)
                    for u in tasks(ACT_STEPS, s, *when):
                        q, qpar = chunk_of(u, c, par)
                        of = ("DT", u[1]) if u[0] == "ABS" else u
                        i = use_no(of, c, when) if of[0] in ("IN", "Z", "GT", "BC", "DT", "RX") else None
                        before = use_no(("Z", u[1] - 1), c, when) if u[0] == "Z" and u[1] > 0 else None
                        if u == ("TANH", KI - 1):
                            before = use_no(("Z", TS - 1), c, when)
                        if u[0] in AFTER:
                            after.scalar_task(act, u, q, i)
                        else:
                            task(u, q, qpar, i, before)

            chunks(act, body)

        @block.gpsimd
        def _(pool):
            def times_u(q, qpar, half):
                pool.wait_ge(dt_done, KI * q + MH * (half + 1))
                wait(pool, dbu_done, SW * (q - 1) + NST * (half + 1))
                r = slice(MH * half, MH * (half + 1))
                pool.tensor_tensor(dtu[:, r, :], dt[:, qpar, r, :], u_sb[:, r, :], ALU.mult).then_inc(dtu_done, 1)

            def times_b(c, s):
                n, half = s % NST, s // NST
                if n == 0:
                    pool.wait_ge(dtu_done, 2 * c + half + 1)
                if half == 0:
                    pool.wait_ge(bb_landed[n], 16 * (c + 1))
                wait(pool, scan_done, MH * (SW * c + s - 1))
                pool.tensor_tensor(dbu[:, s % 2], dtu[:, MH * half:MH * (half + 1), :],
                                   bb[:, n, :].unsqueeze(1).to_broadcast([P, MH, CH]), ALU.mult).then_inc(dbu_done, 1)

            after.pad_regions(pool)
            times_u(0, 0, 0)

            def body(c, par, when):
                ahead, behind, late = when
                for s in range(SW):
                    if ahead and s == SW - 1:
                        times_u(c + 1, 1 - par, 0)
                    times_b(c, s)
                    if s == 1:
                        times_u(c, par, 1)
                    for u in tasks(POOL_STEPS, s, *when):
                        after.pool_task(pool, u, *chunk_of(u, c, par))

            chunks(pool, body)

        @block.vector
        def _(ve):
            def task(u, q, qpar, i):
                kind, m = u
                b = bank(u)
                if kind == "CONV":
                    conv_tap(q, m)
                elif kind == "SILU":
                    ve.wait_ge(tanh_u, KI * q + m + 1)
                    ve.scalar_tensor_tensor(u_sb[:, m, :], scr[:, m, :], 1.0, u_sb[:, m, :],
                                            ALU.add, ALU.mult).then_inc(u_done, 1)
                elif kind == "BC":
                    bc_parts(q, qpar, b, i)
                elif kind == "SOFT":
                    ve.wait_ge(soft_log, KI * q + m + 1)
                    ve.scalar_tensor_tensor(dt[:, qpar, m, :], vb[:, m, :], 0.0, scr[:, m, :],
                                            ALU.max, ALU.add).then_inc(dt_done, 1)
                elif kind == "GATE":
                    ve.wait_ge(ytr_done, SW * q + NST * (m + 1))
                    for t in range(TS):
                        ve.tensor_tensor(g[:, t, m * HD:(m + 1) * HD], y_ps[:, t, :], zg[:, t, m * HD:(m + 1) * HD],
                                         ALU.mult).then_inc(g_done, 1)
                elif kind == "Z":
                    ve.wait_ge(tanh_z, TS * q + m + 1)
                    ve.scalar_tensor_tensor(zg[:, m, :], thz[:], 1.0, px[:, b, :], ALU.add, ALU.mult).then_inc(px_free[b], 1)

            def conv_tap(q, k):
                for m in range(KI):
                    if k == 1:
                        ve.wait_ge(tap0_done, KI * q + m + 1)
                    else:
                        ve.wait_ge(conv_step, KI * (TAPS - 1) * q + KI * (k - 2) + m + 1)
                    ve.scalar_tensor_tensor(u_sb[:, m, :], xin[:, m, k:k + CH], w_conv[:, m, k:k + 1], u_sb[:, m, :],
                                            ALU.mult, ALU.add).then_inc(conv_step, 1)
                if k == TAPS - 1:
                    ve.wait_ge(conv_step, KI * (TAPS - 1) * (q + 1))
                    ve.tensor_copy(xin[:, :, 0:TAPS - 1], xin[:, :, CH:CH + TAPS - 1]).then_inc(head_done, 1)

            def bc_parts(q, par, b, i):
                lo, lo2 = slice(BC, 2 * BC), slice(2 * BC, 3 * BC)
                ve.wait_ge(bc_hi, q + 1)
                for r in (lo, lo2):
                    last = ve.tensor_tensor(bcr[r], px[r, b, :], bc3[r, par, :], ALU.subtract)
                last.then_inc(px_free[b], 1)
                ve.wait_ge(px_free[b], i + 1)
                for r in (lo, lo2):
                    last = ve.tensor_copy(bc3[r, par, :], bcr[r])
                last.then_inc(bc_step, 1)
                ve.wait_ge(bc_step, 3 * q + 1)
                ve.tensor_tensor(bcr[lo2], bcr[lo2], bc3[lo2, par, :], ALU.subtract).then_inc(bc_step, 1)
                ve.wait_ge(bc_step, 3 * q + 2)
                ve.tensor_copy(bc3[lo2, par, :], bcr[lo2]).then_inc(bc_step, 1)

            def scans(c, s):
                n, m0 = s % NST, s // NST * MH
                ve.wait_ge(dbu_done, SW * c + s + 1)
                for m in range(MH):
                    ve.wait_ge(da_full, MH * (SW * c + s) + m + 1)
                    ve.tensor_tensor_scan(h[:, s % HR, m, :], da_ps[:, m, :], dbu[:, s % 2, m, :],
                                          carry[:, n, m0 + m:m0 + m + 1], ALU.mult, ALU.add).then_inc(scan_done, 1)

            def times_c(c, s):
                ve.wait_ge(cb_full, SW * c + s + 1)
                if isinstance(c, int) and c == NCH - 1 and s == SW - 1:
                    ve.wait_ge(scan_done, MH * SW * NCH)
                ve.tensor_tensor(hc[:, s % 2], h[:, s % HR],
                                 cb_ps[:, s % 2, :].unsqueeze(1).to_broadcast([P, MH, CH]),
                                 ALU.mult).then_inc(hc_done, 1)

            ve.memset(xin[:, :, 0:TAPS - 1], 0.0).then_inc(head_done, 1)
            ve.memset(carry[:], 0.0)
            ve.wait_ge(s_w, 16 * NW)
            ve.tensor_copy(sel[:], sel_f[:]).then_inc(prepv, 1)
            ve.tensor_scalar(w_in[:, :, DI:], w_in[:, :, DI:], 0.5, None, ALU.mult).then_inc(prepv, 1)
            ve.tensor_scalar(w_conv[:], w_conv[:], 0.5, None, ALU.mult).then_inc(prepv, 1)
            ve.tensor_scalar(b_conv[:], b_conv[:], 0.5, None, ALU.mult)
            ve.wait_ge(prep, 1)
            ve.tensor_scalar(a_neg[:], a_neg[:], -1.0, None, ALU.mult).then_inc(prepv, 1)
            ve.wait_ge(prepv, 4)

            for kind, of in (("CONV", range(1, TAPS)), ("SILU", range(KI)), ("BC", range(1)), ("SOFT", range(KI))):
                for m in of:
                    task((kind, m), 0, 0, use_no(("BC", 0), "prologue", None) if kind == "BC" else None)
            after.vector_constants(ve)

            def body(c, par, when):
                behind = when[1]
                for s in range(SW):
                    scans(c, s)
                    for u in tasks(VE_STEPS, s, *when):
                        kind, m = u
                        if kind == "GATE" and m == 1:
                            if behind:
                                task(u, c - 1, 1 - par, None)
                            continue
                        q, qpar = chunk_of(u, c, par)
                        i = None
                        if kind == "STATS":
                            i = [use_no(("OUT", v), c, when) for v in (0, 1)]
                        elif kind in ("OUT", "BC", "LG"):
                            i = use_no(u, c, when)
                        elif kind == "PLACE":
                            i = use_no(("RK", m), c, when)
                        if kind in AFTER:
                            after.vector_task(ve, u, q, qpar, i)
                        else:
                            task(u, q, qpar, i)
                    if s > 0:
                        times_c(c, s - 1)
                    elif behind:
                        times_c(c - 1, SW - 1)

            chunks(ve, body)
            times_c(NCH - 1, SW - 1)
            task(("GATE", 1), NCH - 1, 1, None)



GR = 4


def experts(nc, A, out, after):
    LAG = 3
    HALVES = 2
    with ExitStack() as ctx:
        def sb(name, shape, dt=F32):
            return ctx.enter_context(nc.sbuf_tensor(name, shape, dt))

        def sem(name):
            return ctx.enter_context(nc.semaphore(name))

        g, gT, x1T, px, ident = after.g, after.gT, after.x1T, after.px, after.ident
        wgu = sb("wgu", [P, E, KD, 2 * EI])
        wd = sb("wd", [P, E, D])
        sgu = sb("sgu", [P, HALVES, KD, 2 * EI])
        sd = sb("sd", [P, HALVES, D])
        xall = sb("xall", [P, NT, D])
        tile_no = sb("tile_no", [P, 2])
        beyond = sb("beyond", [P, NTILE])
        onef = sb("onef", [P, E])
        cnt = sb("cnt", [P, 8, E])
        cnt_i = sb("cnt_i", [P, E], I32)
        tab = sb("tab", [P, 6, 2])
        tab_i = sb("tab_i", [P, 2, 2], I32)
        tab_row = sb("tab_row", [1, 2, LAG + 2 * P], I32)
        sg = sb("sg", [P, HALVES, CH])
        YR, XR, GB = 8, 4, 8
        gb = wgu[:].rearrange("p e k n -> p (e k n)")[:, 0:GB * TOPK * D].rearrange("p (r k d) -> p r k d", r=GB, k=TOPK)
        place = sb("place", [P, YR], U32)
        weight = sb("weight", [P, YR])
        xg = sb("xg", [P, XR, ROW])
        yb = g[:].rearrange("p t (h d) -> p (t h) d", d=D)
        gT_rows = gT[:].rearrange("p k t -> p (k t)")
        xgT = gT_rows[:, 0:2 * D].rearrange("p (r d) -> p r d", r=2)
        hT = gT_rows[:, 2 * D:3 * D].rearrange("p (r d) -> p r d", r=2)
        hm2 = gT_rows[:, 3 * D:4 * D].rearrange("p (r d) -> p r d", r=2)
        xr_row = after.xr[:].rearrange("p t d -> p (t d)")
        at = 2 * EI
        sg2 = xr_row[:, 0:at].rearrange("p (r d) -> p r d", r=2)
        stats = xr_row[:, at:at + 6 * NT].rearrange("p (j s) -> p j s", s=6)
        mv = xr_row[:, at + 6 * NT:at + 8 * NT].rearrange("p (j s) -> p j s", s=2)
        var, rstd, half, minus, shift = (xr_row[:, at + (8 + i) * NT:at + (9 + i) * NT] for i in range(5))

        ps = ctx.enter_context(nc.psum_tensor("ps", [P, 6, CH], F32))
        gu_ps = ps[:, 0:4].rearrange("p (h a) n -> p h a n", h=HALVES)
        dn_ps = ps[:, 4:6].rearrange("p a n -> p (a n)").rearrange("p (t d) -> p t d", d=D)
        tx_ps = px[:, :, 0:D]
        tg_ps, th_ps, td_ps = (ps[:, 2 * i:2 * i + 2, 0:(P if i == 1 else D)] for i in range(3))

        res_d = nc.dram_tensor("results", (L * TOPK + 2 * E * P, D), F32, kind="Internal").ap()
        tab_d = nc.dram_tensor("tile_table", (2, 2 * P), I32, kind="Internal").ap()

        s_c = sem("constants2_landed")
        s_w = sem("expert_weights_landed")
        s_x = [sem(f"x1_landed{c}") for c in range(NCH)]
        tr_full = sem("tr_full")
        tr_done = sem("tr_done")
        step2 = sem("routing_step2")
        tab_ready = sem("tab_ready")
        tab_stored = sem("tab_stored")
        tab_back = sem("tab_back")
        gu_full = sem("gu_full")
        sg_done = sem("sg_done")
        hm_done = sem("hm_done")
        dn_full = sem("dn_full")
        dn_added = sem("dn_added")
        xg_landed = [sem(f"xg_landed{i}") for i in range(XR)]
        tx_full = sem("tx_full")
        xgT_done = sem("xgT_done")
        tg_full = sem("tg_full")
        tsg_done = sem("tile_silu_done")
        thm_done = sem("tile_product_done")
        th_full = sem("th_full")
        hT_done = sem("hT_done")
        td_full = sem("td_full")
        y_done = sem("y_done")
        y_stored = [sem(f"y_stored{i}") for i in range(YR)]
        places_done = sem("places_done")
        gathered = [sem(f"gathered{i}") for i in range(GB)]
        thirds = sem("thirds_added")
        halved = sem("halved")
        added = sem("added")
        ln_step = sem("ln2_step")
        var_done = sem("var2_done")
        rstd_done = sem("rstd2_done")
        pow_done = sem("pow_done")
        out_done = sem("out_done")
        s_out = sem("out_written")
        EARLY = 2
        assert NTILE % 8 == 0
        last_q, last_par = NCH - 1, 1

        def last_use(u):
            return use_no(u, "epilogue", None)

        block = ctx.enter_context(nc.Block())

        def pipeline(eng, step, peeled=1):
            for i in range(8 * peeled):
                step(i, i % 8)
            with eng.Fori(peeled, NTILE // 8) as k:
                for r in range(8):
                    step(8 * k + r, r)
            for i in range(NTILE, NTILE + 8):
                step(i, i - NTILE)

        def valid(i, lag):
            return not isinstance(i, int) or (0 <= i - lag < NTILE)

        def load_many(engine, row, most):
            return nc.values_load_multi_w_load_instructions(
                row, engines=[engine], min_val=0, max_val=most,
                skip_runtime_bounds_check_because="the table is worked out from counts and its tiles end at the last")[1]

        NC = 4
        x1_d, rows_d = after.x1_d, after.rows_d

        def load_x(eng, c):
            eng.wait_ge(after.x1_stored, 16 * (c + 1) + FROM)
            eng.dma_start(xall[:, c * TS:(c + 1) * TS, :],
                          x1_d.rearrange("(j p) d -> p j d", p=P)[:, c * TS:(c + 1) * TS, :]).then_inc(s_x[c], 16)

        @block.sync
        def _(sp):
            for dst, src in (
                (tile_no[:], A["tile_no"]),
                (beyond[:], A["tiles"].partition_broadcast(P)),
                (sgu[:], A["sguT"].rearrange("h (k p) n -> p h k n", p=P)),
                (sd[:], A["sdT"].rearrange("h p n -> p h n")),
            ):
                sp.dma_start(dst, src).then_inc(s_c, 16)

            for c in range(EARLY):
                load_x(sp, c)
            gu_d = A["guT"].rearrange("e (k p) n -> p e k n", p=P)
            d_d = A["dT"].rearrange("e p n -> p e n")
            for e in range(0, E, 4):
                sp.dma_start(wgu[:, e:e + 4], gu_d[:, e:e + 4]).then_inc(s_w, 16)
                sp.dma_start(wd[:, e:e + 4], d_d[:, e:e + 4]).then_inc(s_w, 16)
            after.store_rows(sp, last_q, last_par)
            sp.wait_ge(tab_ready, 1)
            for a in range(2):
                sp.dma_start(tab_d[a].rearrange("(c p) -> p c", p=P), tab_i[:, a, :],
                             allow_slow_non_contiguous=True).then_inc(tab_stored, 16)
            sp.wait_ge(tab_stored, 32)
            sp.dma_start(tab_row[:, :, LAG:], tab_d.unsqueeze(0)).then_inc(tab_back, 16)
            sp.wait_ge(tab_back, 16)
            for par in range(2):
                sp.wait_ge(after.scattered[par], 16 * TS * TOPK * NCH // 2 + 16)

            first_rows = []

            def step(i, r):
                if r == 0:
                    first_rows[:] = load_many(mybir.EngineType.SP, tab_row[0:1, 1, bass.ds(LAG + i, 8)], E * CAP - P)
                if valid(i, 0):
                    wait(sp, tx_full, i - XR + 1)
                    sp.sem_inc(after.seen, 1)
                    wait(sp, places_done, i - XR + 1)
                    sp.dma_start(xg[:, r % XR, :], rows_d[bass.ds(first_rows[r], P), :]).then_inc(xg_landed[r % XR], 16)
                if isinstance(i, int) and EARLY <= i < NCH:
                    load_x(sp, i)

            pipeline(sp, step)
            for r in range(YR):
                sp.wait_ge(y_stored[r], 16 * (NTILE // YR))
            for j in range(NT):
                wait(sp, added, 2 * (j - GB + 1))
                sp.dma_start(gb[:, j % GB], res_d[j * P * TOPK:(j + 1) * P * TOPK].rearrange("(p k) d -> p k d", p=P)
                             ).then_inc(gathered[j % GB], 16)
            o_d = out.rearrange("(j p) d -> p j d", p=P)
            for j in range(0, NT, GR):
                sp.wait_ge(out_done, j + GR)
                sp.dma_start(o_d[:, j:j + GR, :], xall[:, j:j + GR, :]).then_inc(s_out, 16)
            sp.wait_ge(s_out, 16 * (NT // GR))

        @block.tensor
        def _(pe):
            for u in EPILOGUE:
                after.tensor_use(pe, u, last_q, last_par, last_use(u), transposes_of(u, "epilogue", None))
            for v in (0, 1):
                pe.wait_ge(after.px_free[v], last_use(("TOTAL", 1) if v else ("RK", 0)) + 1)
            pe.wait_ge(s_c, 16 * NC)

            def transposed(c):
                pe.wait_ge(s_x[c], 16)
                wait(pe, tr_done, KD * c)
                for k in range(KD):
                    for t in range(TS):
                        mm = pe.transpose(px[:, k, t * P:(t + 1) * P], xall[:, c * TS + t, k * P:(k + 1) * P], ident[:])
                    mm.then_inc(tr_full, 1)

            def shared(c, another):
                pe.wait_ge(tr_done, KD * (c + 1))
                for half in range(HALVES):
                    wait(pe, hm_done, HALVES * (c - 1) + half + 1)
                    for a in range(2):
                        for k in range(KD):
                            mm = pe.matmul(gu_ps[:, half, a, :], sgu[:, half, k, a * EI:(a + 1) * EI],
                                           x1T[:, k, :], start=(k == 0), stop=(k == KD - 1))
                        mm.then_inc(gu_full, 1)
                if another:
                    transposed(c + 1)
                pe.wait_ge(hm_done, HALVES * (c + 1))
                wait(pe, dn_added, c)
                for t in range(TS):
                    for half in range(HALVES):
                        mm = pe.matmul(dn_ps[:, t, :], sg[:, half, t * P:(t + 1) * P], sd[:, half, :],
                                       start=(half == 0), stop=(half == HALVES - 1))
                mm.then_inc(dn_full, 1)

            transposed(0)
            for c in range(EARLY):
                shared(c, c + 1 < EARLY)
            pe.wait_ge(dn_added, EARLY)
            pe.wait_ge(s_w, 16 * 2 * (E // 4))
            pe.wait_ge(tab_back, 16)

            experts_of = []

            def step(i, r):
                if r == 0:
                    experts_of[:] = load_many(mybir.EngineType.PE, tab_row[0:1, 0, bass.ds(i, 8 + LAG)], E - 1)
                if valid(i, 0):
                    """x of tile i, transposed"""
                    pe.wait_ge(xg_landed[r % XR], 16 * (i // XR + 1) if isinstance(i, int) else (i - r % XR) * 4 + 16)
                    wait(pe, xgT_done, i - 1)
                    for k in range(KD):
                        mm = pe.transpose(tx_ps[:, r % 2, k * P:(k + 1) * P], xg[:, r % XR, k * P:(k + 1) * P], ident[:])
                    mm.then_inc(tx_full, 1)
                if valid(i, 1):
                    """gate and up of tile i - 1"""
                    q = (r + 1) % 2
                    e = experts_of[r + LAG - 1]
                    pe.wait_ge(xgT_done, i)
                    wait(pe, thm_done, i - 2)
                    for k in range(KD):
                        mm = pe.matmul(tg_ps[:, q, :], xgT[:, q, k * P:(k + 1) * P], wgu[:, bass.ds(e, 1), k, :],
                                       start=(k == 0), stop=(k == KD - 1))
                    mm.then_inc(tg_full, 1)
                if valid(i, 2):
                    """the product of tile i - 2, transposed"""
                    q = r % 2
                    pe.wait_ge(thm_done, i - 1)
                    wait(pe, hT_done, i - 3)
                    pe.transpose(th_ps[:, q, :], hm2[:, q, :], ident[:]).then_inc(th_full, 1)
                if valid(i, 3):
                    """the result of tile i - 3"""
                    q = (r + 1) % 2
                    e = experts_of[r + LAG - 3]
                    pe.wait_ge(hT_done, i - 2)
                    wait(pe, y_done, i - 4)
                    pe.matmul(td_ps[:, q, :], hT[:, q, :], wd[:, bass.ds(e, 1), :], start=True, stop=True).then_inc(td_full, 1)

            pipeline(pe, step)
            pe.wait_ge(y_done, NTILE)
            transposed(EARLY)
            for c in range(EARLY, NCH):
                shared(c, c + 1 < NCH)

        @block.scalar
        def _(act):
            for m in range(KI):
                after.scalar_task(act, ("GT", m), last_q, last_use(("GT", m)))
            for m in range(KD):
                after.scalar_task(act, ("RX", m), last_q, last_use(("RX", m)))
            after.scalar_task(act, ("PROB", 0), last_q, None)

            def copies(c):
                for k in range(KD):
                    act.wait_ge(tr_full, KD * c + k + 1)
                    wait(act, gu_full, 2 * HALVES * c)
                    act.activation(x1T[:, k, :], px[:, k, :], ACT.Copy).then_inc(tr_done, 1)

            def shared(c, another):
                for half in range(HALVES):
                    act.wait_ge(gu_full, 2 * (HALVES * c + half) + 1)
                    wait(act, dn_full, c)
                    act.activation(sg[:, half, :], gu_ps[:, half, 0, :], ACT.Silu).then_inc(sg_done, 1)
                if another:
                    copies(c + 1)

            copies(0)
            for c in range(EARLY):
                shared(c, c + 1 < EARLY)
            act.wait_ge(dn_full, EARLY)

            def step(i, r):
                if valid(i, 0):
                    act.wait_ge(tx_full, i + 1)
                    wait(act, tg_full, i - 1)
                    act.activation(xgT[:, r % 2, :], tx_ps[:, r % 2, :], ACT.Copy).then_inc(xgT_done, 1)
                if valid(i, 1):
                    q = (r + 1) % 2
                    act.wait_ge(tg_full, i)
                    wait(act, thm_done, i - 2)
                    act.activation(sg2[:, q, :], tg_ps[:, q, 0:EI], ACT.Silu).then_inc(tsg_done, 1)

            pipeline(act, step)

            def normalise(g):
                act.wait_ge(rstd_done, g + 1)
                for j in range(g * GR, (g + 1) * GR):
                    act.activation(xall[:, j, :], xall[:, j, :], ACT.Identity, bias=shift[:, j:j + 1],
                                   scale=rstd[:, j:j + 1]).then_inc(out_done, 1)

            copies(EARLY)
            done = EARLY
            for g in range(NT // GR):
                while done < min(GR // TS * (g + 1) + EARLY + 1, NCH):
                    shared(done, done + 1 < NCH)
                    done += 1
                normalise(g)

        @block.gpsimd
        def _(pool):
            def ln_rstd(g):
                pool.wait_ge(var_done, g + 1)
                r = slice(g * GR, (g + 1) * GR)
                pool.tensor_tensor(rstd[:, r], var[:, r], half[:, r], ALU.pow).then_inc(pow_done, 1)
                pool.wait_ge(pow_done, g + 1)
                pool.tensor_tensor(shift[:, r], minus[:, r], rstd[:, r], ALU.mult).then_inc(rstd_done, 1)

            for m in range(TS * TOPK):
                if m == TS * TOPK // 2 + 1:
                    after.pool_task(pool, ("RSTD", 0), last_q, last_par)
                after.pool_task(pool, ("SCATTER", m), last_q - 1, 1 - last_par)
            for m in range(TS * TOPK):
                after.pool_task(pool, ("SCATTER", m), last_q, last_par)

            def step(i, r):
                if valid(i, LAG):
                    slot = (r - LAG) % YR
                    pool.wait_ge(y_done, i - LAG + 1)
                    pool.sem_inc(after.seen, 1)
                    pool.indirect_dma_start(res_d, bass.IndirectOffsetOnAxis(place[:, slot:slot + 1], 0),
                                            yb[:, slot, :], None).then_inc(y_stored[slot], 16)

            pipeline(pool, step)
            for j in range(NT):
                pool.wait_ge(gathered[j % GB], 16 * (j // GB + 1))
                pool.tensor_tensor(gb[:, j % GB, 0:TOPK // 2], gb[:, j % GB, 0:TOPK // 2], gb[:, j % GB, TOPK // 2:],
                                   ALU.add).then_inc(thirds, 1)
                pool.wait_ge(thirds, j + 1)
                pool.tensor_tensor(gb[:, j % GB, 0], gb[:, j % GB, 0], gb[:, j % GB, 1], ALU.add).then_inc(halved, 1)
                if j % GR == 2 and j > GR:
                    ln_rstd(j // GR - 1)
            ln_rstd(NT // GR - 1)

        @block.vector
        def _(ve):
            n = [0]

            def then(ins):
                n[0] += 1
                ins.then_inc(step2, 1)
                ve.wait_ge(step2, n[0])
                ve.sem_inc(after.seen, 1)

            def rows(a):
                return a.unsqueeze(2).to_broadcast([P, NT, E])

            def cols(a):
                return a.unsqueeze(1).to_broadcast([P, NT, E])

            ve.memset(onef[:], 1.0)
            ve.memset(tab_row[:, :, 0:LAG], 0)
            for u, of in ((("OUT", 0), ("OUT", 0)), (("OUT", 1), ("OUT", 1)), (("STATS", 0), None), (("NORM", 0), None),
                          (("LG", 1), ("LG", 1)), (("CHOOSE", 0), None), (("PLACE", 0), ("RK", 0))):
                i = [last_use(("OUT", v)) for v in (0, 1)] if u[0] == "STATS" else last_use(of) if of else None
                after.vector_task(ve, u, last_q, last_par, i)

            def product(c):
                for half in range(HALVES):
                    s = HALVES * c + half
                    ve.wait_ge(sg_done, s + 1)
                    ve.wait_ge(gu_full, 2 * s + 2)
                    ve.tensor_tensor(sg[:, half, :], sg[:, half, :], gu_ps[:, half, 1, :], ALU.mult).then_inc(hm_done, 1)

            def add_shared(c):
                ve.wait_ge(dn_full, c + 1)
                ve.tensor_tensor(xall[:, c * TS:(c + 1) * TS, :], xall[:, c * TS:(c + 1) * TS, :], dn_ps[:],
                                 ALU.add).then_inc(dn_added, 1)

            C, N_, INC, EXC, V, BOTH, LE = (cnt[:, i, :] for i in range(7))
            ve.wait_ge(after.px_full[1], last_use(("TOTAL", 1)) + 1)
            then(ve.tensor_copy(C, px[:, 1, 0:E]))
            ve.wait_ge(s_c, 16 * NC)
            then(ve.tensor_scalar(cnt_i[:], C, float(P - 1), None, ALU.add))
            ve.sem_inc(after.px_free[1], 1)
            then(ve.tensor_scalar(cnt_i[:], cnt_i[:], P.bit_length() - 1, None, ALU.arith_shift_right))
            then(ve.tensor_copy(N_, cnt_i[:]))
            then(ve.tensor_tensor_scan(INC, onef[:, 0:E], N_, 0.0, ALU.mult, ALU.add))
            then(ve.tensor_tensor(EXC, INC, N_, ALU.subtract))
            then(ve.tensor_scalar(V, INC, -float(P), None, ALU.mult))
            then(ve.tensor_tensor(V, V, C, ALU.add))
            then(ve.tensor_tensor(V, V, after.region[:], ALU.add))
            for c in range(2):
                then(ve.tensor_scalar(BOTH, INC, tile_no[:, c:c + 1], None, ALU.is_le))
                then(ve.tensor_reduce(tab[:, 2, c:c + 1], BOTH, AX.X, ALU.add))
                then(ve.tensor_scalar(LE, EXC, tile_no[:, c:c + 1], None, ALU.is_le))
                then(ve.tensor_tensor(LE, LE, BOTH, ALU.subtract))
                then(ve.tensor_tensor(LE, LE, V, ALU.mult))
                then(ve.tensor_reduce(tab[:, 3, c:c + 1], LE, AX.X, ALU.add))
            then(ve.tensor_scalar(tab[:, 4, :], tile_no[:], float(P), -1.0, ALU.mult, ALU.add))
            then(ve.tensor_tensor(tab[:, 4, :], tab[:, 4, :], tab[:, 3, :], ALU.add))
            tiles = INC[:, E - 1:E]
            then(ve.tensor_scalar(tab[:, 0, :], tile_no[:], tiles, None, ALU.is_lt))
            then(ve.tensor_scalar(tab[:, 4, :], tab[:, 4, :], -float((E - 1) * CAP), None, ALU.add))
            then(ve.tensor_tensor(tab[:, 4, :], tab[:, 4, :], tab[:, 0, :], ALU.mult))
            then(ve.tensor_scalar(tab_i[:, 0, :], tab[:, 2, :], float(E - 1), None, ALU.min))
            ve.tensor_scalar(tab_i[:, 1, :], tab[:, 4, :], float((E - 1) * CAP), None, ALU.add).then_inc(tab_ready, 1)
            then(ve.tensor_scalar(beyond[:], beyond[:], tiles, -1.0, ALU.subtract, ALU.subtract))
            then(ve.tensor_scalar(beyond[:], beyond[:], 0.0, float(P), ALU.max, ALU.mult))
            for c in range(EARLY):
                product(c)
                add_shared(c)
            ve.memset(half, -0.5)
            ve.wait_ge(tab_back, 16)
            of_tile = []

            def step(i, r):
                if r == 0:
                    of_tile[:] = load_many(mybir.EngineType.DVE, tab_row[0:1, 0, bass.ds(i, 8 + LAG)], E - 1)
                if valid(i, 1):
                    slot, x_slot, e = (r - 1) % YR, (r - 1) % XR, of_tile[r + LAG - 1]
                    ve.wait_ge(xg_landed[x_slot], 16 * ((i - 1) // XR + 1) if isinstance(i, int)
                               else (i - 1 - x_slot) * 4 + 16)
                    ve.sem_inc(after.seen, 1)
                    if not (isinstance(i, int) and i - 1 < YR):
                        ve.wait_ge(y_stored[slot], 16 * ((i - 1) // YR) if isinstance(i, int) else (i - 1 - slot) * 2)
                    ve.tensor_tensor(place[:, slot:slot + 1], xg[:, x_slot, bass.ds(e + D, 1)],
                                     beyond[:, bass.ds(i - 1, 1)], ALU.add)
                    ve.tensor_copy(weight[:, slot:slot + 1], xg[:, x_slot, bass.ds(e + (D + E), 1)]).then_inc(places_done, 1)
                if valid(i, 1):
                    q = (r + 1) % 2
                    ve.wait_ge(tsg_done, i)
                    wait(ve, th_full, i - 2)
                    ve.tensor_tensor(hm2[:, q, :], sg2[:, q, :], tg_ps[:, q, EI:2 * EI], ALU.mult).then_inc(thm_done, 1)
                if valid(i, 2):
                    ve.wait_ge(th_full, i - 1)
                    wait(ve, td_full, i - 3)
                    ve.tensor_copy(hT[:, r % 2, :], th_ps[:, r % 2, :]).then_inc(hT_done, 1)
                if valid(i, 3):
                    q = (r + 1) % 2
                    slot = (r + 5) % YR
                    ve.wait_ge(td_full, i - 2)
                    ve.wait_ge(places_done, i - 2)
                    ve.tensor_scalar(yb[:, slot, :], td_ps[:, q, :], weight[:, slot:slot + 1], None,
                                     ALU.mult).then_inc(y_done, 1)

            pipeline(ve, step, peeled=2)

            for j in range(NT):
                if j % TS == 1 and j // TS + EARLY < NCH:
                    product(j // TS + EARLY)
                if j % TS == 3 and j // TS + EARLY < NCH:
                    add_shared(j // TS + EARLY)
                if j % TS == 0:
                    ve.wait_ge(dn_added, j // TS + 1)
                ve.wait_ge(halved, j + 1)
                for k in (0, 2):
                    if k > 0:
                        ve.wait_ge(added, 2 * j + 1)
                    ve.tensor_tensor(xall[:, j, :], xall[:, j, :], gb[:, j % GB, k, :], ALU.add).then_inc(added, 1)
                ve.wait_ge(added, 2 * (j + 1))
                ve.bn_stats(stats[:, j, :], xall[:, j, :]).then_inc(ln_step, 1)
                ve.wait_ge(ln_step, 2 * j + 1)
                ve.bn_aggr(mv[:, j, :], stats[:, j, :]).then_inc(ln_step, 1)
                if j % GR == GR - 1:
                    g = slice(j + 1 - GR, j + 1)
                    ve.wait_ge(ln_step, 2 * j + 2)
                    ve.tensor_scalar(minus[:, g], mv[:, g, 0], -1.0, None, ALU.mult)
                    ve.tensor_scalar(var[:, g], mv[:, g, 1], LN_EPS, None, ALU.add).then_inc(var_done, 1)



def build(nc, A, out):
    with ExitStack() as ctx:
        after = AfterScan(nc, ctx, A)
        mamba(nc, A, after)
        experts(nc, A, out, after)


def kernel(**inputs):
    import numpy as np
    import concourse.bacc as bacc
    from concourse.bass_utils import run_bass_kernel_spmd

    def T(a):
        return np.swapaxes(np.asarray(a), -1, -2)

    w = {k.replace("L0_attn_", "").replace("L0_ffn_", ""): np.asarray(v) for k, v in inputs.items()}
    x = w["x"].reshape(L, D)
    sgu = np.concatenate([w["shared_gate_w"].reshape(2, EI, D), w["shared_up_w"].reshape(2, EI, D)], 1)
    arrays = {
        "x": x, "xT": T(x), "W_inT": T(w["W_in"]), "W_dtT": T(w["W_dt"]), "W_outT": T(w["W_out"]),
        "W_BC3T": T(np.concatenate([w["W_B"], w["W_C"]] * 3)), "W_conv": w["W_conv"].reshape(DI, TAPS),
        "b_conv": w["b_conv"].reshape(KI, P).T, "b_dt": w["b_dt"].reshape(KI, P).T, "A_log": w["A_log"],
        "router_T": T(w["router_weight"]), "router_bias": w["e_score_bias"],
        "guT": T(w["gate_up_proj"]), "dT": T(w["down_proj"]),
        "sguT": T(sgu), "sdT": T(w["shared_down_w"]).reshape(2, EI, D),
        "region1": (np.arange(E) * CAP + P + 1).astype(np.float32),
        "place0": (TOPK * np.arange(CH, dtype=np.float32) - 1).reshape(TS, P).T,
        "pads": np.concatenate([np.zeros((P, D)), L * TOPK + np.arange(P)[:, None] + P * np.arange(E),
                                np.zeros((P, E))], 1).astype(np.float32),
        "tiles": np.arange(NTILE, dtype=np.float32),
        "tile_no": np.arange(2 * P, dtype=np.float32).reshape(2, P).T,
        "before": np.triu(np.ones((P, P), np.float32), 1),
        "ident": np.eye(P, dtype=np.float32), "sel3": np.tile(np.eye(BC, dtype=np.float32), (3, 1)),
    }
    arrays = {k: np.ascontiguousarray(v) for k, v in arrays.items()}
    nc = bacc.Bacc("TRN2", target_bir_lowering=False, num_devices=1)
    A = {k: nc.dram_tensor(k + "_d", v.shape, F32, kind="ExternalInput").ap() for k, v in arrays.items()}
    out = nc.dram_tensor("out_d", (L, D), F32, kind="ExternalOutput").ap()
    build(nc, A, out)
    r = run_bass_kernel_spmd(nc, [{k + "_d": v for k, v in arrays.items()}], core_ids=[0])
    return np.asarray(r.results[0]["out_d"]).reshape(1, L, D)
```
